# Optimizing a Trainium2 kernel written in Bass

```python
import numpy as np
import jax
import jax.numpy as jnp

def _softmax(x, axis=-1):
    return jax.nn.softmax(x, axis=axis)

def _gelu(x):
    return jax.nn.gelu(x, approximate=True)

def _silu(x):
    return jax.nn.silu(x)

def _sigmoid(x):
    return jax.nn.sigmoid(x)

def _layernorm(x, axis=-1, eps=1e-05):
    m = jnp.mean(x, axis=axis, keepdims=True)
    v = jnp.var(x, axis=axis, keepdims=True)
    return (x - m) / jnp.sqrt(v + eps)

def _scatter_add(tgt, idx, src, axis=0):
    return tgt.at[idx].add(src)

def _segment_sum(src, seg, n):
    return jax.ops.segment_sum(src, seg, n)
kernel_name = 'mk_xattn_ffn_d1_seqx_r4_3168fa'

def setup_inputs(seed: int=0):
    np.random.seed(seed)
    _w = jnp.asarray

    def _rec_inputs():
        import jax
        import jax.numpy as jnp
        _rk = jax.random.key(seed)
        x = -0.0002928 + 1 * jax.random.normal(jax.random.fold_in(_rk, 1), (8, 256, 256), jnp.float32)
        _lenS = 256 - jax.random.randint(jax.random.fold_in(_rk, 7), (8,), 0, max(1, 256 // 4) + 1, jnp.int32)
        _lenS2 = 77 - jax.random.randint(jax.random.fold_in(_rk, 8), (8,), 0, max(1, 77 // 4) + 1, jnp.int32)
        _ctx_1024P = jax.random.normal(jax.random.fold_in(_rk, 11), (8, 16, 256), jnp.float32)
        _ctx_1024c = jax.random.dirichlet(jax.random.fold_in(_rk, 511), 0.3 * jnp.ones((16,), jnp.float32), (8, 77))
        _ctx_1024t = jnp.einsum('bsk,bkd->bsd', _ctx_1024c, _ctx_1024P)
        _ctx_1024t = _ctx_1024t * jax.lax.rsqrt(jnp.mean(jnp.square(_ctx_1024t)) + 1e-12) * 0.953939
        ctx_1024 = -1.39393e-06 + 0.999914 * (_ctx_1024t + 0.3 * jax.random.normal(jax.random.fold_in(_rk, 611), (8, 77, 256), jnp.float32))
        _validS = jnp.arange(256)[None, :] < _lenS[:, None]
        _validS2 = jnp.arange(77)[None, :] < _lenS2[:, None]
        _causal = jnp.tril(jnp.ones((256, 256), dtype=bool))
        mask_BxSxS2_ik1 = jnp.where(jnp.broadcast_to(_validS2[:, None, :], (8, 256, 77)), 1, 0).astype(jnp.int32)
        return (x, ctx_1024, mask_BxSxS2_ik1)
    x, ctx_1024, mask_BxSxS2_ik1 = _rec_inputs()

    def _L0_xattn_setup():
        import jax, jax.numpy as jnp
        import numpy as np
        B, S, D, H = (2, 512, 256, 16)
        HD = D // H
        key = jax.random.key(seed)
        ks = jax.random.split(key, 12)
        s = 1.0 / np.sqrt(D)
        return {'query': jax.random.normal(ks[0], (B, S, D), jnp.float32), 'key': jax.random.normal(ks[1], (B, S, D), jnp.float32), 'value': jax.random.normal(ks[2], (B, S, D), jnp.float32), 'mask': jax.random.randint(ks[3], (B, S, S), 0, 2, jnp.int32), 'wq_kernel': jax.random.normal(ks[4], (D, D), jnp.float32) * s, 'wq_bias': jnp.zeros((D,), jnp.float32), 'wk_kernel': jax.random.normal(ks[5], (D, D), jnp.float32) * s, 'wk_bias': jnp.zeros((D,), jnp.float32), 'wv_kernel': jax.random.normal(ks[6], (D, D), jnp.float32) * s, 'wv_bias': jnp.zeros((D,), jnp.float32), 'wo_kernel': jax.random.normal(ks[7], (D, D), jnp.float32) * s, 'wo_bias': jnp.zeros((D,), jnp.float32)}
    _L0_xattn_all = _L0_xattn_setup()
    _L0_xattn_in = {k: v for k, v in _L0_xattn_all.items() if k in ('wq_kernel', 'wq_bias', 'wk_kernel', 'wk_bias', 'wv_kernel', 'wv_bias', 'wo_kernel', 'wo_bias')}
    del _L0_xattn_all

    def _L0_ffn_setup():
        import math
        import jax, jax.numpy as jnp
        import numpy as np
        E = 8
        TOPK = 2
        CF = 1.25
        EPS = 1e-05
        NEG = -1e+30

        def _layer_norm(x, gamma, beta):
            mu = jnp.mean(x, axis=-1, keepdims=True)
            var = jnp.mean((x - mu) ** 2, axis=-1, keepdims=True)
            return (x - mu) * jax.lax.rsqrt(var + EPS) * gamma + beta
        key = jax.random.key(seed)
        ks = jax.random.split(key, 8)
        B, S, H, F = (4, 512, 256, 1024)
        hidden_states = jax.random.normal(ks[0], (B, S, H), jnp.float32)
        token_mask = jnp.ones((B, S), jnp.int32)
        Wr = jax.random.normal(ks[1], (H, E), jnp.float32) * 0.001
        br = jnp.zeros((E,), jnp.float32)
        W1 = jax.random.normal(ks[2], (E, H, F), jnp.float32) * (1.0 / np.sqrt(H))
        b1 = jax.random.normal(ks[3], (E, F), jnp.float32) * 0.01
        W2 = jax.random.normal(ks[4], (E, F, H), jnp.float32) * (1.0 / np.sqrt(F))
        b2 = jax.random.normal(ks[5], (E, H), jnp.float32) * 0.01
        gamma = jnp.ones((H,), jnp.float32)
        beta = jnp.zeros((H,), jnp.float32)
        return {'hidden_states': hidden_states, 'Wr': Wr, 'br': br, 'W1': W1, 'b1': b1, 'W2': W2, 'b2': b2, 'gamma': gamma, 'beta': beta, 'token_mask': token_mask}
    _L0_ffn_all = _L0_ffn_setup()
    _L0_ffn_in = {k: v for k, v in _L0_ffn_all.items() if k in ('Wr', 'br', 'W1', 'b1', 'W2', 'b2', 'gamma', 'beta', 'token_mask')}
    del _L0_ffn_all
    return {'x': x, 'ctx_1024': ctx_1024, 'mask_BxSxS2_ik1': mask_BxSxS2_ik1, 'L0_xattn_wq_kernel': _L0_xattn_in['wq_kernel'], 'L0_xattn_wq_bias': _L0_xattn_in['wq_bias'], 'L0_xattn_wk_kernel': _L0_xattn_in['wk_kernel'], 'L0_xattn_wk_bias': _L0_xattn_in['wk_bias'], 'L0_xattn_wv_kernel': _L0_xattn_in['wv_kernel'], 'L0_xattn_wv_bias': _L0_xattn_in['wv_bias'], 'L0_xattn_wo_kernel': _L0_xattn_in['wo_kernel'], 'L0_xattn_wo_bias': _L0_xattn_in['wo_bias'], 'L0_ffn_Wr': _L0_ffn_in['Wr'], 'L0_ffn_br': _L0_ffn_in['br'], 'L0_ffn_W1': _L0_ffn_in['W1'], 'L0_ffn_b1': _L0_ffn_in['b1'], 'L0_ffn_W2': _L0_ffn_in['W2'], 'L0_ffn_b2': _L0_ffn_in['b2'], 'L0_ffn_gamma': _L0_ffn_in['gamma'], 'L0_ffn_beta': _L0_ffn_in['beta'], 'L0_ffn_token_mask': _L0_ffn_in['token_mask']}

def reference(x, ctx_1024, mask_BxSxS2_ik1, L0_xattn_wq_kernel, L0_xattn_wq_bias, L0_xattn_wk_kernel, L0_xattn_wk_bias, L0_xattn_wv_kernel, L0_xattn_wv_bias, L0_xattn_wo_kernel, L0_xattn_wo_bias, L0_ffn_Wr, L0_ffn_br, L0_ffn_W1, L0_ffn_b1, L0_ffn_W2, L0_ffn_b2, L0_ffn_gamma, L0_ffn_beta, L0_ffn_token_mask):
    import jax
    import jax.numpy as jnp

    def _L0_xattn_ref(query, key, value, mask, wq_kernel, wq_bias, wk_kernel, wk_bias, wv_kernel, wv_bias, wo_kernel, wo_bias):
        import jax, jax.numpy as jnp
        import numpy as np
        B, S, D, H = (2, 512, 256, 16)
        HD = D // H
        b = query.shape[0]

        def split_heads(x):
            return x.reshape(b, -1, H, HD).transpose(0, 2, 1, 3)
        q = split_heads(query @ wq_kernel + wq_bias)
        k = split_heads(key @ wk_kernel + wk_bias)
        v = split_heads(value @ wv_kernel + wv_bias)
        scores = jnp.einsum('bhqd,bhkd->bhqk', q, k) / jnp.sqrt(jnp.float32(HD))
        m = mask[:, None, :, :]
        scores = jnp.where(m == 0, jnp.float32(-1000000000.0), scores)
        attn = jax.nn.softmax(scores, axis=-1)
        out = jnp.einsum('bhqk,bhkd->bhqd', attn, v)
        out = out.transpose(0, 2, 1, 3).reshape(b, -1, D)
        return out @ wo_kernel + wo_bias

    def _L0_ffn_ref(hidden_states, Wr, br, W1, b1, W2, b2, gamma, beta, token_mask):
        import math
        import jax, jax.numpy as jnp
        import numpy as np
        E = 8
        TOPK = 2
        CF = 1.25
        EPS = 1e-05
        NEG = -1e+30

        def _layer_norm(x, gamma, beta):
            mu = jnp.mean(x, axis=-1, keepdims=True)
            var = jnp.mean((x - mu) ** 2, axis=-1, keepdims=True)
            return (x - mu) * jax.lax.rsqrt(var + EPS) * gamma + beta
        B, S, H = hidden_states.shape
        x = hidden_states.reshape(-1, H)
        N = x.shape[0]
        logits = x @ Wr + br
        top_vals, top_idx = jax.lax.top_k(logits, TOPK)
        w = jax.nn.softmax(top_vals, axis=-1)
        flat_idx = top_idx.reshape(-1)
        flat_tok = jnp.repeat(jnp.arange(N), TOPK)
        w_flat = w.reshape(-1)
        cap = max(int(math.ceil(N / E * CF)), 1)
        key_mat = jnp.where(flat_idx[None, :] == jnp.arange(E)[:, None], w_flat[None, :], NEG)
        kv, ki = jax.lax.top_k(key_mat, cap)
        valid = kv > NEG / 2
        tok = flat_tok[ki]
        gate = jnp.where(valid, w_flat[ki], 0.0)
        xe = x[tok]
        h1 = jnp.einsum('ech,ehf->ecf', xe, W1) + b1[:, None, :]
        h1 = jax.nn.gelu(h1, approximate=False)
        y = jnp.einsum('ecf,efh->ech', h1, W2) + b2[:, None, :]
        out = jnp.zeros_like(x).at[tok.reshape(-1)].add((y * gate[..., None]).reshape(-1, H))
        out = out.reshape(B, S, H) + hidden_states
        return _layer_norm(out, gamma, beta)
    x = x + _L0_xattn_ref(_layernorm(x, axis=-1), ctx_1024, ctx_1024, mask_BxSxS2_ik1, L0_xattn_wq_kernel, L0_xattn_wq_bias, L0_xattn_wk_kernel, L0_xattn_wk_bias, L0_xattn_wv_kernel, L0_xattn_wv_bias, L0_xattn_wo_kernel, L0_xattn_wo_bias)
    x = x + _L0_ffn_ref(_layernorm(x, axis=-1), L0_ffn_Wr, L0_ffn_br, L0_ffn_W1, L0_ffn_b1, L0_ffn_W2, L0_ffn_b2, L0_ffn_gamma, L0_ffn_beta, L0_ffn_token_mask)
    return x

_drawn_inputs = setup_inputs


def setup_inputs(seed=0):
    import zlib

    import numpy as np

    out = dict(_drawn_inputs(seed))
    spreads = {'L0_xattn_wq_bias': (0.0, 0.283),
     'L0_xattn_wk_bias': (0.0, 2.0),
     'L0_xattn_wv_bias': (0.0, 0.1),
     'L0_xattn_wo_bias': (0.0, 0.1),
     'L0_ffn_br': (0.0, 0.1),
     'L0_ffn_gamma': (1.0, 0.2),
     'L0_ffn_beta': (0.0, 0.1)}
    factors = {'L0_ffn_b1': 63.268, 'L0_ffn_b2': 44.882}
    for name, (base, spread) in spreads.items():
        noise = np.random.default_rng([zlib.crc32(name.encode()), seed]).standard_normal(out[name].shape)
        drawn = base * np.exp(spread * noise) if base else spread * noise
        out[name] = jnp.asarray(drawn.astype(out[name].dtype))
    for name, factor in factors.items():
        out[name] = (out[name] * factor).astype(out[name].dtype)
    return out
```

```python
from contextlib import ExitStack

import concourse.bass as bass
from concourse import mybir

F32 = mybir.dt.float32
BF16 = mybir.dt.bfloat16
F16 = mybir.dt.float16
I32 = mybir.dt.int32
ALU = mybir.AluOpType
ACT = mybir.ActivationFunctionType
AX = mybir.AxisListType

P = 128
EPS = 1e-5
MASKED = -(2.0 ** 40)
UNASSIGNED = -1000.0
SATURATED = 16.635532
GONE = -110.0


class Batch:

    def __init__(self, loop, offset):
        self.loop, self.offset = loop, offset
        self.n = 2 * loop + offset
        self.par = offset % 2
        self.turn = loop + offset // 2

    def plus(self, k):
        return Batch(self.loop, self.offset + k)


def wait(engine, semaphore, value):
    if isinstance(value, int) and value <= 0:
        return
    engine.wait_ge(semaphore, value)


def batches(engine, count, before, body):
    before(Batch(0, 0))
    body(Batch(0, 0), True, False)
    with engine.Fori(0, (count - 2) // 2) as loop:
        body(Batch(loop, 1), False, False)
        body(Batch(loop, 2), False, False)
    body(Batch(0, count - 1), False, True)


def xattn_moe(nc, x, ctx, mask, wq, bq, wk, bk, wv, bv, wo, bo, wr, br, w1, b1, w2, b2,
              gamma, beta, out):
    B, S, D = x.shape
    SK = ctx.shape[1]
    H = 16
    HD = D // H
    E, _, F = w1.shape
    N = B * S
    CAP = max(-(-N * 5 // (E * 4)), 1)
    T = S // P
    NT = N // P
    KD = D // P
    KF = F // P
    G = D // P
    SLOTS = [(m * P, min(P, CAP - m * P)) for m in range(-(-CAP // P))]
    NM = len(SLOTS)
    RB = 32
    J = P // RB
    assert T == 2 and G == 2 and HD * 2 == RB and NT * E == P and B % 2 == 0

    z_table = nc.dram_tensor("z_table", (N, D), F32, kind="Internal").ap()
    acc_table = nc.dram_tensor("acc_table", (N + CAP, D), F32, kind="Internal").ap()

    with ExitStack() as stack:
        def sb(name, shape, dt=F32):
            return stack.enter_context(nc.sbuf_tensor(name, shape, dt))

        def ps(name, shape, dt=F32):
            return stack.enter_context(nc.psum_tensor(name, shape, dt))

        def sem(name):
            return stack.enter_context(nc.semaphore(name))

        score_ps = ps("score_ps", [P, J, 512])
        max_ps = ps("max_ps", [P, 2, 512])
        bank_a = ps("bank_a", [P, 512])
        bank_b = ps("bank_b", [P, 512])
        y_ps = (max_ps[:, 0, 0:D], max_ps[:, 1, 0:D], bank_a[:, 0:D])

        wq_sb, wk_sb, wv_sb, wo_sb = (sb(n, [P, KD, D]) for n in ("wq_sb", "wk_sb", "wv_sb", "wo_sb"))
        wr_sb = sb("wr_sb", [P, KD, E])
        bqk_rows = sb("bqk_rows", [4, P])
        bqk = sb("bqk", [P, 4])
        bv_bc, bo_bc, gamma_bc, beta_bc = (sb(n, [P, D]) for n in ("bv_bc", "bo_bc", "gamma_bc", "beta_bc"))
        br_bc = sb("br_bc", [P, E])
        ident = sb("ident", [P, P])
        ident_bf = sb("ident_bf", [P, P], BF16)
        part_i = sb("part_i", [P, 4], I32)
        part_f = sb("part_f", [P, 4])
        expert_of_p = sb("expert_of_p", [P, 2])
        shift_rows = sb("shift_rows", [P, H, SK], BF16)
        half_ones = sb("half_ones", [P, 2, RB])
        minus_half = sb("minus_half", [P, 2])
        eps = sb("eps", [P, 2])
        zero_rows = sb("zero_rows", [P, CAP * D // P])

        x_in = sb("x_in", [P, 2, T, D])
        mask_in = sb("mask_in", [P, 2, T, SK], I32)
        ctx_in = sb("ctx_in", [SK, 2, D])
        bn1 = sb("bn1", [P, T, 6])
        mv1 = sb("mv1", [P, T, 2])
        rs1 = sb("rs1", [P, T])
        xn = sb("xn", [P, T, D])
        xn_t = sb("xn_t", [P, KD, S])
        ctx_t = sb("ctx_t", [P, KD, SK])
        valid = sb("valid", [P, T, SK])
        any_valid = sb("any_valid", [P, T])
        quarter = sb("quarter", [P, T], BF16)
        quarter_bc = sb("quarter_bc", [P, S])
        mask_and_max = sb("mask_and_max", [P, 2, T, P], BF16)
        shift = sb("shift", [P, S], BF16)
        q_t = sb("q_t", [P, 2, G, S])
        k_t = sb("k_t", [P, 2, G, 2, SK])
        v_pad = sb("v_pad", [SK, 2, H, RB])
        neg_max = sb("neg_max", [P, T, J, 4])
        probs = sb("probs", [SK, 2, J, 2, S])
        recip = sb("recip", [P, S])
        o_t = sb("o_t", [P, G, S])
        x_bo = sb("x_bo", [P, 2, T, D])
        x2 = sb("x2", [P, T, D])
        x2_beta = sb("x2_beta", [P, NT, D])
        bn2 = sb("bn2", [P, T, 6])
        mv2 = sb("mv2", [P, T, 2])
        rs2 = sb("rs2", [P, T])
        z = sb("z", [P, T, D])
        z_t = sb("z_t", [P, KD, S])
        logits = sb("logits", [P, NT, E])

        rank_weight = sb("rank_weight", [P, NT, E])
        col_expert = sb("col_expert", [P, P])
        col_tile = sb("col_tile", [P, P])
        col_index = sb("col_index", [P, P])
        same_expert = sb("same_expert", [P, P], BF16)
        earlier_tile = sb("earlier_tile", [P, P], BF16)
        same_tile = sb("same_tile", [P, P], BF16)
        earlier_expert = sb("earlier_expert", [P, P], BF16)
        top = sb("top", [P, 2, NT])
        hit = sb("hit", [P, NT, E])
        first = sb("first", [P, NT])
        chosen = sb("chosen", [P, 2, NT, E])
        rest = sb("rest", [P, NT, E])
        gap = sb("gap", [P, NT])
        pair = sb("pair", [P, 3, NT, E])
        keys = sb("keys", [P, NT, E])
        gate_of = sb("gate_of", [P, 4, NT])
        gates = sb("gates", [P, NT, E])
        keys_flat = sb("keys_flat", [P, P])
        gates_flat = sb("gates_flat", [P, P])
        junk = sb("junk", [P, 3, P], BF16)
        junk3 = sb("junk3", [P, 3])
        digits = sb("digits", [P, 15, 3], I32)
        candidates = sb("candidates", [P, 3], I32)
        counts = sb("counts", [P, 3])
        counts_bf = sb("counts_bf", [P, 3], BF16)
        digit = sb("digit", [P, 4])
        prefix = sb("prefix", [P, 2], I32)
        flips = sb("flips", [P, 3], I32)
        above = sb("above", [P, P])
        equal = sb("equal", [P, P])
        zeros_row = sb("zeros_row", [P, P])
        order_of = sb("order_of", [P, P])
        taken = sb("taken", [P, P])
        stats = sb("stats", [P, 8])
        stats_bf = sb("stats_bf", [P, 4], BF16)
        slot_flat = sb("slot_flat", [P, P])
        active = sb("active", [P, 8])
        active_bf = sb("active_bf", [P, 1], BF16)
        to_position = sb("to_position", [P, P])
        order_rows = sb("order_rows", [E, 2, E])
        order_i = sb("order_i", [1, E + 1], I32)
        slot_of = sb("slot_of", [P, NT, E + 2])
        gate_rest = sb("gate_rest", [P, 2, NT, E])

        slot_number = sb("slot_number", [P, CAP], F16)
        token_info = sb("token_info", [P, NT, E + 2, 6], BF16)
        one_hot = sb("one_hot", [P, 2, NT, CAP], BF16)
        spare_row = sb("spare_row", [P, NM])
        slot_info = sb("slot_info", [P, 2, NM, 6])
        slot_calc = sb("slot_calc", [P, 2, 3, NM])
        slot_gate = sb("slot_gate", [P, 2, NM])
        source_row = sb("source_row", [P, 2, NM], I32)
        target_row = sb("target_row", [P, 2, NM], I32)
        w1_sb = sb("w1_sb", [P, 2, KD, F])
        w2_sb = sb("w2_sb", [P, 2, KF, D])
        b1_rows = sb("b1_rows", [KF, 2, P])
        b1_t = sb("b1_t", [P, 2, KF])
        b2_bc = sb("b2_bc", [P, 2, D])
        xe = sb("xe", [P, 2, NM, D])
        xe_t = sb("xe_t", [P, KD, CAP])
        hidden = sb("hidden", [P, KF, CAP])
        y_b2 = sb("y_b2", [P, NM, D])
        y_out = sb("y_out", [P, 2, NM, D])

        acc = w1_sb[:].rearrange("p a k f -> p (a k f)").rearrange("p (t d) -> p t d", d=D)
        bn3 = sb("bn3", [P, 2, T, 6])
        mv3 = sb("mv3", [P, 2, T, 2])
        rs3 = sb("rs3", [P, 2, T])
        nb3 = sb("nb3", [P, 2, T])
        normed = sb("normed", [P, 2, T, D])
        scaled = sb("scaled", [P, 2, T, D])
        result = sb("result", [P, 2, T, D])

        ld_w = [sem(f"ld_w{k}") for k in range(5)]
        ld_x, ld_mask, ld_ctx = ([sem(f"{n}{p}") for p in range(2)] for n in ("ld_x", "ld_mask", "ld_ctx"))
        ld_bias, ld_w1, ld_w2 = ([sem(f"{n}{p}") for p in range(2)] for n in ("ld_bias", "ld_w1", "ld_w2"))
        ld_acc = [sem(f"ld_acc{p}") for p in range(B)]
        st_z, st_zero, st_out = sem("st_z"), sem("st_zero"), [sem("st_out0"), sem("st_out1")]
        pool_const, dve_const, act_const = sem("pool_const"), sem("dve_const"), sem("act_const")
        bqk_ps, bqk_ok = sem("bqk_ps"), sem("bqk_ok")
        s_bn1, s_mv1, s_add1, s_rs1, s_xn, s_xbo = (sem(n) for n in ("bn1_ok", "mv1_ok", "add1_ok", "rs1_ok", "xn_ok", "xbo_ok"))
        s_valid, s_mask, s_quarter = sem("valid_ok"), sem("mask_ok"), sem("quarter_ok")
        p_ctx, e_ctx, p_xnt, e_xnt, p_q, e_q, p_kv, e_kv = (sem(n) for n in (
            "ctx_t_ps", "ctx_t_ok", "xn_t_ps", "xn_t_ok", "q_ps", "q_ok", "kv_ps", "kv_ok"))
        p_max, e_max, s_max, s_hi, s_lo, p_shift, e_shift = (sem(n) for n in (
            "max_ps_ok", "max_taken", "max_ok", "max_hi_ok", "max_lo_ok", "shift_ps", "shift_ok"))
        p_score, e_exp, p_pv, e_recip, e_o = (sem(n) for n in (
            "scores_ps", "probs_ok", "pv_ps", "recip_ok", "o_t_ok"))
        p_o, e_x2, s_bn2, s_mv2, s_add2, s_rs2, s_x2b, e_z, p_zt, e_zt, p_lg, e_lg = (sem(n) for n in (
            "o_ps", "x2_ok", "bn2_ok", "mv2_ok", "add2_ok", "rs2_ok", "x2_beta_ok", "z_ok", "z_t_ps",
            "z_t_ok", "logits_ps", "logits_ok"))
        dve_b = sem("dve_b")
        keys_ready, keys_ps, keys_ok, e_ok, gates_ready, gates_ps, gates_ok = (sem(n) for n in (
            "keys_ready", "keys_ps", "keys_ok", "exp_gap_ok", "gates_ready", "gates_ps", "gates_ok"))
        counted, summed = sem("counted"), sem("summed")
        order_ready = sem("order_ready")
        gate_pos_ps, gate_pos_ok, slot_pos_ps, slot_pos_ok = (sem(n) for n in (
            "gate_pos_ps", "gate_pos_ok", "slot_pos_ps", "slot_pos_ok"))
        gate_split = sem("gate_split")
        s_hot, p_info, e_info, s_calc, s_rows = (sem(n) for n in (
            "one_hot_ok", "slot_info_ps", "slot_info_ok", "slot_calc_ok", "rows_ok"))
        gathered = [[sem(f"gathered{p}_{m}") for m in range(NM)] for p in range(2)]
        p_xe, e_xe, p_b1, e_b1, p_h, e_h, p_y, e_y, s_y, scattered = (sem(n) for n in (
            "xe_t_ps", "xe_t_ok", "b1_ps", "b1_ok", "h_ps", "h_ok", "y_ps", "y_b2_ok", "y_ok", "scattered"))
        experts_done = sem("experts_done")
        d_bn, d_mv, d_add, d_rs, d_nb, d_norm, d_gamma, d_res = (sem(n) for n in (
            "d_bn", "d_mv", "d_add", "d_rs", "d_nb", "d_norm", "d_gamma", "d_res"))

        POOL_CONSTS = 19
        x_by_tile = x.rearrange("b (t p) d -> b p t d", p=P)
        out_by_tile = out.rearrange("b (t p) d -> b p t d", p=P)
        mask_by_tile = mask.rearrange("b (t p) k -> b p t k", p=P)
        z_rows = z_table.rearrange("(b t p) d -> b p t d", t=T, p=P)
        acc_rows = acc_table[0:N].rearrange("(b t p) d -> b p t d", t=T, p=P)
        spare_rows = acc_table[N:N + CAP].rearrange("r d -> (r d)").rearrange("(p c) -> p c", p=P)

        def head_column(g, j, s):
            return 4 * j + 2 * g + s

        block = stack.enter_context(nc.Block())

        @block.sync
        def _(sp):
            def load_batch(b):
                wait(sp, s_xbo, b.n - 1)
                wait(sp, s_xn, b.n - 1)
                sp.dma_start(x_in[:, b.par], x_by_tile[b.n]).then_inc(ld_x[b.par], 16)
                wait(sp, s_valid, b.n - 1)
                sp.dma_start(mask_in[:, b.par], mask_by_tile[b.n]).then_inc(ld_mask[b.par], 16)
                wait(sp, p_ctx, b.n - 1)
                sp.dma_start(ctx_in[:, b.par], ctx[b.n]).then_inc(ld_ctx[b.par], 16)

            def store_z(b):
                wait(sp, e_z, b.n + 1)
                sp.dma_start(z_rows[b.n], z[:]).then_inc(st_z, 16)
                sp.dma_start(acc_rows[b.n], z[:]).then_inc(st_z, 16)

            def before(b):
                load_batch(b)
                sp.dma_start(wq_sb[:], wq.rearrange("(k p) n -> p k n", p=P)).then_inc(ld_w[0], 16)
                sp.dma_start(bqk_rows[0:2], bq.rearrange("(g p) -> g p", p=P)).then_inc(ld_w[0], 16)
                sp.dma_start(bqk_rows[2:4], bk.rearrange("(g p) -> g p", p=P)).then_inc(ld_w[0], 16)
                sp.dma_start(wk_sb[:], wk.rearrange("(k p) n -> p k n", p=P)).then_inc(ld_w[1], 16)
                sp.dma_start(wv_sb[:], wv.rearrange("(k p) n -> p k n", p=P)).then_inc(ld_w[2], 16)
                sp.dma_start(bv_bc[:], bv.partition_broadcast(P)).then_inc(ld_w[2], 16)
                load_batch(b.plus(1))
                sp.dma_start(wo_sb[:], wo.rearrange("(k p) n -> p k n", p=P)).then_inc(ld_w[3], 16)
                sp.dma_start(bo_bc[:], bo.partition_broadcast(P)).then_inc(ld_w[3], 16)
                sp.dma_start(wr_sb[:], wr.rearrange("(k p) n -> p k n", p=P)).then_inc(ld_w[4], 16)
                sp.dma_start(br_bc[:], br.partition_broadcast(P)).then_inc(ld_w[4], 16)
                sp.dma_start(gamma_bc[:], gamma.partition_broadcast(P)).then_inc(ld_w[4], 16)
                sp.dma_start(beta_bc[:], beta.partition_broadcast(P)).then_inc(ld_w[4], 16)
                wait(sp, pool_const, POOL_CONSTS)
                sp.dma_start(spare_rows, zero_rows[:]).then_inc(st_zero, 16)

            def body(b, is_first, is_last):
                if not is_first:
                    if not is_last:
                        load_batch(b.plus(1))
                    store_z(b.plus(-1))

            batches(sp, B, before, body)
            store_z(Batch(0, B - 1))

            sp.wait_ge(order_ready, 1)
            n_active = sp.value_load(order_i[0:1, E:E + 1], min_val=2, max_val=E)

            def load_expert(i, par):
                e = sp.value_load(order_i[0:1, bass.ds(i, 1)], min_val=0, max_val=E - 1)
                of = bass.ds(e, 1)
                sp.dma_start(b1_rows[:, par], b1[of].rearrange("e (k p) -> k (e p)", p=P)).then_inc(ld_bias[par], 16)
                sp.dma_start(b2_bc[:, par], b2[of].partition_broadcast(P).rearrange("p e d -> p (e d)")).then_inc(ld_bias[par], 16)
                sp.dma_start(w1_sb[:, par], w1[of].rearrange("e (k p) f -> p (e k) f", p=P)).then_inc(ld_w1[par], 16)
                sp.dma_start(w2_sb[:, par], w2[of].rearrange("e (k p) d -> p (e k) d", p=P)).then_inc(ld_w2[par], 16)

            load_expert(0, 0)
            load_expert(1, 1)
            with sp.Fori(0, (E - 2) // 2) as loop:
                for par in range(2):
                    i = 2 * loop + par
                    with sp.If(i + 2 < n_active):
                        sp.wait_ge(s_y, NM * (i + 1))
                        load_expert(i + 2, par)

            sp.wait_ge(experts_done, 1)
            for b in range(B):
                sp.dma_start(acc[:, T * b:T * b + T], acc_rows[b]).then_inc(ld_acc[b], 16)
            with sp.Fori(0, B // 2) as loop:
                for par in range(2):
                    b = Batch(loop, par)
                    sp.wait_ge(d_res, b.n + 1)
                    sp.dma_start(out_by_tile[b.n], result[:, par]).then_inc(st_out[par], 16)
            for par in range(2):
                sp.wait_ge(st_out[par], 16 * (B // 2))

        @block.gpsimd
        def _(pool):
            made = [0]

            def const(ins, then=False):
                ins.then_inc(pool_const, 1)
                made[0] += 1
                if then:
                    pool.wait_ge(pool_const, made[0])

            const(nc.gpsimd.memset(ident[:], 0.0), True)
            const(nc.gpsimd.affine_select(out=ident[:], in_=ident[:], compare_op=ALU.not_equal, fill=1.0,
                                          base=0, pattern=[[-1, P]], channel_multiplier=1))
            const(nc.gpsimd.iota(part_i[:, 0:1], pattern=[[0, 1]], base=0, channel_multiplier=1))
            const(nc.gpsimd.memset(minus_half[:], -0.5))
            const(nc.gpsimd.memset(eps[:], EPS))
            const(nc.gpsimd.memset(mask_and_max[:], 0.0))
            const(nc.gpsimd.memset(shift_rows[:], 0.0), True)
            const(nc.gpsimd.affine_select(out=shift_rows[:], in_=shift_rows[:], compare_op=ALU.not_equal, fill=1.0,
                                          base=0, pattern=[[0, H], [-1, SK]], channel_multiplier=1), True)
            const(nc.gpsimd.affine_select(out=shift_rows[:], in_=shift_rows[:], compare_op=ALU.not_equal, fill=1.0,
                                          base=-(P - 2 * H), pattern=[[-1, H], [0, SK]], channel_multiplier=1), True)
            const(nc.gpsimd.affine_select(out=shift_rows[:], in_=shift_rows[:], compare_op=ALU.not_equal, fill=1.0,
                                          base=-(P - H), pattern=[[-1, H], [0, SK]], channel_multiplier=1))
            const(nc.gpsimd.memset(v_pad[:], 0.0))
            const(nc.gpsimd.memset(half_ones[:], 0.0), True)
            const(nc.gpsimd.memset(half_ones[:, 0, 0:HD], 1.0))
            const(nc.gpsimd.memset(half_ones[:, 1, HD:RB], 1.0))
            const(nc.gpsimd.memset(zero_rows[:], 0.0))
            imprecise = dict(allow_small_or_imprecise_dtypes=True)
            const(nc.gpsimd.iota(col_expert[:], pattern=[[0, NT], [1, E]], base=0, channel_multiplier=0, **imprecise))
            const(nc.gpsimd.iota(col_tile[:], pattern=[[1, NT], [0, E]], base=0, channel_multiplier=0, **imprecise))
            const(nc.gpsimd.iota(col_index[:], pattern=[[1, P]], base=0, channel_multiplier=0, **imprecise))
            const(nc.gpsimd.iota(rank_weight[:], pattern=[[0, NT], [-1, E]], base=E, channel_multiplier=0, **imprecise))
            assert made[0] == POOL_CONSTS

            def scale_of(mv, rs, have_mv, added, have_rs, count):
                wait(pool, have_mv, count)
                nc.gpsimd.tensor_tensor(rs[:], mv[:, :, 1], eps[:], ALU.add).then_inc(added, 1)
                wait(pool, added, count)
                nc.gpsimd.tensor_tensor(rs[:], rs[:], minus_half[:], ALU.pow).then_inc(have_rs, 1)

            def front(b):
                wait(pool, s_xn, b.n)
                scale_of(mv1, rs1, s_mv1, s_add1, s_rs1, b.n + 1)
                pool.wait_ge(ld_w[3], 32)
                wait(pool, e_x2, b.n - 1)
                pool.wait_ge(ld_x[b.par], 16 * (b.turn + 1))
                nc.gpsimd.tensor_tensor(x_bo[:, b.par], x_in[:, b.par],
                                        bo_bc[:].unsqueeze(1).to_broadcast([P, T, D]), ALU.add).then_inc(s_xbo, 1)

            def back(b):
                wait(pool, e_z, b.n)
                scale_of(mv2, rs2, s_mv2, s_add2, s_rs2, b.n + 1)
                pool.wait_ge(ld_w[4], 64)
                nc.gpsimd.tensor_tensor(x2_beta[:, bass.ds(T * b.n, T)], x2[:],
                                        beta_bc[:].unsqueeze(1).to_broadcast([P, T, D]), ALU.add).then_inc(s_x2b, 1)

            def body(b, is_first, is_last):
                if not is_first:
                    back(b.plus(-1))
                if not is_last:
                    front(b.plus(1))

            batches(pool, B, front, body)
            back(Batch(0, B - 1))

            nc.gpsimd.iota(slot_number[:], pattern=[[1, CAP]], base=1, channel_multiplier=0, **imprecise).then_inc(pool_const, 1)
            nc.gpsimd.iota(token_info[:, :, :, 0], pattern=[[1, NT], [0, E + 2]], base=0, channel_multiplier=0, **imprecise).then_inc(pool_const, 1)
            nc.gpsimd.iota(token_info[:, :, :, 1], pattern=[[0, NT], [0, E + 2]], base=0, channel_multiplier=1, **imprecise).then_inc(pool_const, 1)
            nc.gpsimd.memset(token_info[:, :, :, 2:6], 1.0).then_inc(pool_const, 1)
            nc.gpsimd.iota(spare_row[:], pattern=[[P, NM]], base=N, channel_multiplier=1, **imprecise).then_inc(pool_const, 1)
            nc.gpsimd.memset(slot_of[:], 0.0).then_inc(pool_const, 1)

            last_z_row, last_acc_row = pool.to_reg(N - 1), pool.to_reg(N + CAP - 1)

            def gather(i, par):
                pool.wait_ge(s_rows, i + 1)
                for m, (_, rows) in enumerate(SLOTS):
                    nc.gpsimd.indirect_dma_start(
                        xe[0:rows, par, m], None, z_table,
                        bass.IndirectOffsetOnAxis(ap=source_row[0:rows, par, m:m + 1], axis=0),
                        bounds_check=last_z_row, oob_is_err=False).then_inc(gathered[par][m], 16)

            pool.wait_ge(st_z, 32 * B)
            pool.wait_ge(st_zero, 16)
            gather(0, 0)
            gather(1, 1)
            pool.wait_ge(order_ready, 1)
            n_active = pool.value_load(order_i[0:1, E:E + 1], min_val=2, max_val=E)
            for i in range(E):
                par = i % 2
                with pool.If(i < n_active):
                    for m, (_, rows) in enumerate(SLOTS):
                        pool.wait_ge(s_y, NM * i + m + 1)
                        nc.gpsimd.indirect_dma_start(
                            acc_table, bass.IndirectOffsetOnAxis(ap=target_row[0:rows, par, m:m + 1], axis=0),
                            y_out[0:rows, par, m], None, bounds_check=last_acc_row, oob_is_err=True,
                            compute_op=ALU.add).then_inc(scattered, 16)
                    pool.wait_ge(scattered, 16 * NM * (i + 1))
                if i + 2 < E:
                    with pool.If(i + 2 < n_active):
                        pool.wait_ge(p_xe, i + 1)
                        gather(i + 2, par)
            nc.gpsimd.memset(junk3[:], 0.0).then_inc(experts_done, 1)

            with pool.Fori(0, B // 2) as loop:
                for par in range(2):
                    b = Batch(loop, par)
                    pool.wait_ge(d_mv, b.n + 1)
                    nc.gpsimd.tensor_tensor(rs3[:, par], mv3[:, par, :, 1], eps[:], ALU.add).then_inc(d_add, 1)
                    pool.wait_ge(d_add, b.n + 1)
                    nc.gpsimd.tensor_tensor(rs3[:, par], rs3[:, par], minus_half[:], ALU.pow).then_inc(d_rs, 1)
                    pool.wait_ge(d_norm, b.n + 1)
                    nc.gpsimd.tensor_tensor(scaled[:, par], normed[:, par],
                                            gamma_bc[:].unsqueeze(1).to_broadcast([P, T, D]), ALU.mult).then_inc(d_gamma, 1)

        @block.scalar
        def _(act):
            act.wait_ge(pool_const, POOL_CONSTS)
            nc.scalar.copy(ident_bf[:], ident[:]).then_inc(act_const, 1)
            act.wait_ge(bqk_ps, 1)
            nc.scalar.copy(bqk[:], bank_a[:, 0:4]).then_inc(bqk_ok, 1)

            def ctx_and_quarter(b):
                wait(act, p_kv, b.n)
                wait(act, e_q, 2 * b.n)
                act.wait_ge(p_ctx, b.n + 1)
                nc.scalar.copy(ctx_t[:], bank_b[:, 0:KD * SK].rearrange("p (k c) -> p k c", k=KD)).then_inc(e_ctx, 1)
                nc.scalar.copy(quarter_bc[:], bank_b[:, S:2 * S]).then_inc(e_ctx, 1)

            def xn_transposed(b):
                wait(act, p_q, b.n)
                act.wait_ge(p_xnt, b.n + 1)
                nc.scalar.copy(xn_t[:].rearrange("p k s -> p (k s)"), bank_a[:]).then_inc(e_xnt, 1)

            def exponentials(b, g):
                act.wait_ge(p_score, G * b.n + g + 1)
                wait(act, p_pv, G * (b.n - 1) + g + 1)
                nc.scalar.activation(probs[:, g].rearrange("k j s q -> k (j s q)"),
                                     score_ps[0:SK].rearrange("k j c -> k (j c)"), ACT.Exp).then_inc(e_exp, 1)

            def z_transposed(b):
                wait(act, p_lg, b.n)
                act.wait_ge(p_zt, b.n + 1)
                nc.scalar.copy(z_t[:].rearrange("p k s -> p (k s)"), bank_a[:]).then_inc(e_zt, 1)

            def body(b, is_first, is_last):
                if not is_last:
                    ctx_and_quarter(b.plus(1))
                if not is_last:
                    xn_transposed(b.plus(1))
                act.wait_ge(p_shift, b.n + 1)
                nc.scalar.copy(shift[:], bank_b[:, 0:S // 2].bitcast(BF16)).then_inc(e_shift, 1)
                exponentials(b, 0)
                if not is_first:
                    z_transposed(b.plus(-1))
                exponentials(b, 1)

            def before(b):
                ctx_and_quarter(b)
                xn_transposed(b)

            batches(act, B, before, body)
            z_transposed(Batch(0, B - 1))

            act.wait_ge(keys_ready, 1)
            nc.scalar.activation(gate_of[:, 0], gap[:], ACT.Exp, scale=-1.0).then_inc(e_ok, 1)
            act.wait_ge(keys_ps, 1)
            nc.scalar.copy(keys_flat[:], bank_a[:, 0:P]).then_inc(keys_ok, 1)
            act.wait_ge(gates_ps, 1)
            nc.scalar.copy(gates_flat[:], bank_b[:, 0:P]).then_inc(gates_ok, 1)

            act.wait_ge(order_ready, 1)
            n_active = act.value_load(order_i[0:1, E:E + 1], min_val=2, max_val=E)
            with act.Fori(0, E // 2) as loop:
                for par in range(2):
                    i = 2 * loop + par
                    with act.If(i < n_active):
                        act.wait_ge(p_b1, i + 1)
                        nc.scalar.copy(b1_t[:, par], max_ps[:, 0, 300:300 + KF]).then_inc(e_b1, 1)
                        act.wait_ge(p_xe, i + 1)
                        nc.scalar.copy(xe_t[:, 0], bank_a[:, 0:CAP]).then_inc(e_xe, 1)
                        nc.scalar.copy(xe_t[:, 1], bank_b[:, 0:CAP]).then_inc(e_xe, 1)
                        act.wait_ge(e_b1, i + 1)
                        for k in range(KF):
                            act.wait_ge(p_h, KF * i + k + 1)
                            nc.scalar.activation(hidden[:, k], score_ps[:, k % J, 0:CAP], ACT.Gelu,
                                                 bias=b1_t[:, par, k:k + 1]).then_inc(e_h, 1)

            with act.Fori(0, B // 2) as loop:
                for par in range(2):
                    b = Batch(loop, par)
                    act.wait_ge(d_nb, b.n + 1)
                    for t in range(T):
                        ins = nc.scalar.activation(normed[:, par, t], acc[:, bass.ds(T * b.n + t, 1)].rearrange("p a d -> p (a d)"), ACT.Identity,
                                                   bias=nb3[:, par, t:t + 1], scale=rs3[:, par, t:t + 1])
                    ins.then_inc(d_norm, 1)

        @block.vector
        def _(dve):
            V = nc.vector
            dve.wait_ge(pool_const, POOL_CONSTS)
            made = [0]

            def const(ins, then=False):
                ins.then_inc(dve_const, 1)
                made[0] += 1
                if then:
                    dve.wait_ge(dve_const, made[0])

            const(V.tensor_scalar(part_i[:, 1:2], part_i[:, 0:1], HD, None, ALU.bitwise_and))
            const(V.tensor_scalar(part_i[:, 2:3], part_i[:, 0:1], E - 1, None, ALU.bitwise_and))
            const(V.tensor_scalar(part_i[:, 3:4], part_i[:, 0:1], 3, None, ALU.logical_shift_right), True)
            const(V.tensor_scalar(part_f[:, 1:2], part_i[:, 1:2], 0.0, None, ALU.is_equal))
            const(V.tensor_scalar(part_f[:, 2:3], part_i[:, 1:2], 0.0, None, ALU.not_equal))
            const(V.tensor_copy(expert_of_p[:], part_i[:, 2:4]), True)
            even, odd = part_f[:, 1:2], part_f[:, 2:3]
            HEAD_CONSTS = made[0]

            def front_a(b):
                dve.wait_ge(ld_x[b.par], 16 * (b.turn + 1))
                for t in range(T):
                    V.bn_stats(bn1[:, t], x_in[:, b.par, t]).then_inc(s_bn1, 1)
                dve.wait_ge(ld_mask[b.par], 16 * (b.turn + 1))
                wait(dve, s_rs1, b.n)
                wait(dve, s_xn, b.n)
                dve.wait_ge(s_bn1, T * (b.n + 1))
                for t in range(T):
                    ins = V.tensor_scalar(valid[:, t], mask_in[:, b.par, t], 0.0, 0.0, ALU.not_equal, ALU.max,
                                          accum_out=any_valid[:, t:t + 1])
                ins.then_inc(s_valid, 1)
                for t in range(T):
                    ins = V.bn_aggr(mv1[:, t], bn1[:, t])
                ins.then_inc(s_mv1, 1)
                wait(dve, p_shift, b.n - 1)
                dve.wait_ge(s_valid, b.n + 1)
                wait(dve, p_ctx, b.n)
                for t in range(T):
                    V.tensor_scalar(mask_and_max[:, b.par, t, 0:SK], valid[:, t], any_valid[:, t:t + 1], -MASKED,
                                    ALU.subtract, ALU.mult).then_inc(s_mask, 1)
                V.tensor_scalar(quarter[:], any_valid[:], float(HD) ** -0.5, None, ALU.mult).then_inc(s_quarter, 1)

            def front_xn(b):
                dve.wait_ge(s_rs1, b.n + 1)
                wait(dve, p_xnt, b.n)
                for t in range(T):
                    ins = V.tensor_scalar(xn[:, t], x_in[:, b.par, t], mv1[:, t, 0:1], rs1[:, t:t + 1],
                                          ALU.subtract, ALU.mult)
                ins.then_inc(s_xn, 1)

            def front_q(b):
                dve.wait_ge(p_q, b.n + 1)
                dve.wait_ge(e_ctx, 2 * (b.n + 1))
                for g in range(G):
                    V.scalar_tensor_tensor(q_t[:, b.par, g], bank_a[:, g * S:(g + 1) * S], bqk[:, g:g + 1],
                                           quarter_bc[:], ALU.add, ALU.mult).then_inc(e_q, 1)

            def front_kv(b):
                dve.wait_ge(p_kv, b.n + 1)
                wait(dve, p_pv, G * (b.n - 1))
                for g in range(G):
                    for s, parity in enumerate((even, odd)):
                        V.tensor_scalar(k_t[:, b.par, g, s], bank_a[:, g * SK:(g + 1) * SK], bqk[:, 2 + g:3 + g], parity,
                                        ALU.add, ALU.mult).then_inc(e_kv, 1)
                for s in range(2):
                    V.tensor_tensor(
                        v_pad[:, b.par].rearrange("k (h s) c -> k h s c", s=2)[:, :, s, s * HD:(s + 1) * HD],
                        bank_a[0:SK, S:2 * S].rearrange("k (h s c) -> k h s c", s=2, c=HD)[:, :, s],
                        bv_bc[0:SK].rearrange("k (h s c) -> k h s c", s=2, c=HD)[:, :, s], ALU.add).then_inc(e_kv, 1)

            def take_max(b, k):
                t, half = k // 2, k % 2
                dve.wait_ge(p_max, 4 * b.n + k + 1)
                if k == 0:
                    wait(dve, s_lo, b.n)
                V.tensor_reduce(neg_max[:, t, 2 * half:2 * half + 2],
                                max_ps[:, :, 0:4 * SK].rearrange("p j (c k) -> p j c k", k=SK),
                                AX.X, ALU.max, negate=True).then_inc(e_max, 1)

            def split_max(b):
                negs = neg_max[:].rearrange("p t j c -> p t (j c)")
                dve.wait_ge(e_max, 4 * (b.n + 1))
                V.tensor_copy(mask_and_max[:, b.par, :, P - 2 * H:P - H], negs).then_inc(s_hi, 1)
                dve.wait_ge(s_hi, b.n + 1)
                V.tensor_tensor(mask_and_max[:, b.par, :, P - H:P], negs,
                                mask_and_max[:, b.par, :, P - 2 * H:P - H], ALU.subtract).then_inc(s_lo, 1)

            def normalise(b, g):
                dve.wait_ge(p_pv, G * b.n + g + 1)
                if g == 0:
                    wait(dve, p_o, b.n)
                wait(dve, e_o, 2 * b.n + g)
                V.reciprocal(recip[:], bank_b[:, S:2 * S]).then_inc(e_recip, 1)
                dve.wait_ge(e_recip, 2 * b.n + g + 1)
                V.tensor_tensor(o_t[:, g], bank_b[:, 0:S], recip[:], ALU.mult).then_inc(e_o, 1)

            def back_x2(b):
                dve.wait_ge(p_o, b.n + 1)
                dve.wait_ge(s_xbo, b.n + 1)
                wait(dve, s_x2b, b.n)
                wait(dve, e_z, b.n)
                V.tensor_tensor(x2[:], bank_a[:].rearrange("p (t d) -> p t d", t=T), x_bo[:, b.par], ALU.add).then_inc(e_x2, 1)
                dve.wait_ge(e_x2, b.n + 1)
                for t in range(T):
                    ins = V.bn_stats(bn2[:, t], x2[:, t])
                ins.then_inc(s_bn2, 1)
                dve.wait_ge(s_bn2, b.n + 1)
                wait(dve, s_rs2, b.n)

            def back_mv(b):
                for t in range(T):
                    ins = V.bn_aggr(mv2[:, t], bn2[:, t])
                ins.then_inc(s_mv2, 1)

            def back_z(b):
                dve.wait_ge(s_rs2, b.n + 1)
                wait(dve, p_zt, b.n)
                wait(dve, st_z, 32 * b.n)
                for t in range(T):
                    ins = V.tensor_scalar(z[:, t], x2[:, t], mv2[:, t, 0:1], rs2[:, t:t + 1], ALU.subtract, ALU.mult)
                ins.then_inc(e_z, 1)

            def back_logits(b):
                dve.wait_ge(p_lg, b.n + 1)
                V.tensor_tensor(logits[:, bass.ds(T * b.n, T)], bank_a[:, 0:T * E].rearrange("p (t e) -> p t e", t=T),
                                br_bc[:].unsqueeze(1).to_broadcast([P, T, E]), ALU.add).then_inc(e_lg, 1)

            def before(b):
                front_a(b)
                dve.wait_ge(bqk_ok, 1)
                dve.wait_ge(ld_w[2], 32)
                dve.wait_ge(ld_w[4], 64)
                front_xn(b)
                front_q(b)
                front_kv(b)

            def body(b, is_first, is_last):
                take_max(b, 0)
                if not is_first:
                    back_x2(b.plus(-1))
                take_max(b, 1)
                if not is_first:
                    back_mv(b.plus(-1))
                if not is_last:
                    front_a(b.plus(1))
                take_max(b, 2)
                if not is_last:
                    front_xn(b.plus(1))
                take_max(b, 3)
                split_max(b)
                if not is_first:
                    back_z(b.plus(-1))
                if not is_last:
                    front_q(b.plus(1))
                if not is_first:
                    back_logits(b.plus(-1))
                normalise(b, 0)
                if not is_last:
                    front_kv(b.plus(1))
                normalise(b, 1)

            batches(dve, B, before, body)
            last = Batch(0, B - 1)
            back_x2(last)
            back_mv(last)

            pe_of, pt_of = expert_of_p[:, 0:1], expert_of_p[:, 1:2]
            const(V.tensor_scalar(same_expert[:], col_expert[:], pe_of, None, ALU.is_equal))
            const(V.tensor_scalar(same_tile[:], col_tile[:], pt_of, None, ALU.is_equal))
            const(V.tensor_scalar(earlier_tile[:], col_tile[:], pt_of, None, ALU.is_gt))
            const(V.tensor_scalar(earlier_expert[:], col_expert[:], pe_of, None, ALU.is_gt), True)
            const(V.tensor_tensor(earlier_tile[:], earlier_tile[:], same_expert[:], ALU.mult))
            const(V.tensor_tensor(earlier_expert[:], earlier_expert[:], same_tile[:], ALU.mult))
            const(V.memset(zeros_row[:], 0.0))
            const(V.memset(order_rows[:], 0.0))
            for c in range(3):
                const(V.memset(flips[:, c:c + 1], c + 1))
            dve.wait_ge(dve_const, made[0])
            for r in range(15):
                const(V.tensor_scalar(digits[:, r], flips[:], 2 * (14 - r), None, ALU.logical_shift_left))
            dve.wait_ge(dve_const, made[0])

            back_z(last)
            back_logits(last)

            step = [0]

            def link(ins, then=True):
                ins.then_inc(dve_b, 1)
                step[0] += 1
                if then:
                    dve.wait_ge(dve_b, step[0])

            by_expert = [P, NT, E]

            def bc(a):
                return a.unsqueeze(2).to_broadcast(by_expert)

            dve.wait_ge(e_lg, B)
            for c in range(2):
                src = logits if c == 0 else rest
                link(V.tensor_reduce(top[:, c], src[:], AX.X, ALU.max))
                link(V.tensor_tensor(hit[:], src[:], bc(top[:, c]), ALU.is_equal))
                link(V.tensor_tensor(hit[:], hit[:], rank_weight[:], ALU.mult))
                link(V.tensor_reduce(first[:], hit[:], AX.X, ALU.max))
                link(V.tensor_tensor(chosen[:, c], rank_weight[:], bc(first[:]), ALU.is_equal))
                if c == 0:
                    link(V.scalar_tensor_tensor(rest[:], chosen[:, 0], -1e30, logits[:], ALU.mult, ALU.add))
            link(V.tensor_tensor(gap[:], top[:, 0], top[:, 1], ALU.subtract))
            dve_keys = step[0]
            V.tensor_tensor(pair[:, 0], chosen[:, 0], chosen[:, 1], ALU.add).then_inc(keys_ready, 1)
            link(V.tensor_tensor(pair[:, 1], chosen[:, 0], chosen[:, 1], ALU.subtract))
            dve.wait_ge(keys_ready, 1)
            link(V.tensor_tensor(pair[:, 1], pair[:, 1], bc(gap[:]), ALU.mult))
            link(V.tensor_scalar(pair[:, 1], pair[:, 1], SATURATED, GONE, ALU.min, ALU.max), False)
            link(V.tensor_scalar(pair[:, 2], pair[:, 0], -UNASSIGNED, UNASSIGNED, ALU.mult, ALU.add))
            V.tensor_tensor(keys[:], pair[:, 1], pair[:, 2], ALU.add).then_inc(keys_ready, 1)
            dve.wait_ge(e_ok, 1)
            link(V.tensor_scalar(gate_of[:, 1], gate_of[:, 0], 1.0, None, ALU.add))
            link(V.reciprocal(gate_of[:, 2], gate_of[:, 1]))
            link(V.tensor_tensor(gate_of[:, 3], gate_of[:, 0], gate_of[:, 2], ALU.mult), False)
            link(V.tensor_tensor(gates[:], chosen[:, 0], bc(gate_of[:, 2]), ALU.mult))
            link(V.tensor_tensor(pair[:, 0], chosen[:, 1], bc(gate_of[:, 3]), ALU.mult))
            V.tensor_tensor(gates[:], gates[:], pair[:, 0], ALU.add).then_inc(gates_ready, 1)

            dve.wait_ge(keys_ok, 1)
            link(V.tensor_scalar(junk[:, 0], keys_flat[:], UNASSIGNED / 2, 0.0, ALU.is_gt, ALU.add,
                                 accum_out=active[:, 0:1]))
            V.tensor_copy(active_bf[:], active[:, 0:1]).then_inc(counted, 1)
            dve.wait_ge(summed, 1)
            link(V.tensor_scalar(active[:, 1:2], max_ps[:, 0, 0:1], 0.0, None, ALU.is_gt))
            V.tensor_copy(active_bf[:], active[:, 1:2]).then_inc(counted, 1)
            dve.wait_ge(summed, 2)
            link(V.tensor_copy(active[:, 2:4], max_ps[:, 0, 0:2]))
            link(V.scalar_tensor_tensor(active[:, 4:5], pt_of, float(E), active[:, 2:3], ALU.mult, ALU.add))
            link(V.scalar_tensor_tensor(active[:, 4:5], active[:, 4:5], 1.0, active[:, 1:2], ALU.add, ALU.mult))
            link(V.tensor_scalar(active[:, 4:5], active[:, 4:5], -1.0, None, ALU.add), False)
            link(V.tensor_scalar(order_rows[:, 0], col_index[0:E, 0:E], active[0:E, 2:3], active[0:E, 1:2],
                                 ALU.is_equal, ALU.mult))
            link(V.tensor_scalar(order_rows[:, 0], order_rows[:, 0], expert_of_p[0:E, 0:1], None, ALU.mult))
            V.tensor_scalar(to_position[:], col_index[:], active[:, 4:5], None, ALU.is_equal).then_inc(counted, 1)
            dve.wait_ge(summed, 3)
            link(V.tensor_copy(order_i[0:1, 0:E], max_ps[0:1, 0, 0:E]), False)
            V.tensor_copy(order_i[0:1, E:E + 1], active[0:1, 3:4]).then_inc(order_ready, 1)

            V_first = (-(2.0 - 2.0 ** -23), 0.0, 2.0)
            for c in range(3):
                link(V.tensor_scalar(junk[:, c], keys_flat[:], V_first[c], 0.0, ALU.is_ge, ALU.add,
                                     accum_out=counts[:, c:c + 1]), c == 2)
            V.tensor_copy(counts_bf[:], counts[:]).then_inc(counted, 1)
            dve.wait_ge(summed, 4)
            link(V.tensor_scalar(junk3[:], max_ps[:, 0, 0:3], float(CAP), 0.0, ALU.is_ge, ALU.add,
                                 accum_out=digit[:, 0:1]))
            link(V.tensor_scalar(prefix[:, 0:1], digit[:, 0:1], 2.0, -1.0, ALU.is_lt, ALU.mult), False)
            link(V.tensor_scalar(digit[:, 1:2], digit[:, 0:1], 1.0, None, ALU.is_equal), False)
            link(V.tensor_scalar(digit[:, 2:3], digit[:, 0:1], 3.0, None, ALU.is_equal))
            link(V.tensor_tensor(digit[:, 3:4], digit[:, 1:2], digit[:, 2:3], ALU.add))
            link(V.tensor_scalar(flips[:, 0:1], digit[:, 3:4], 2.0 ** 30, None, ALU.mult))
            link(V.tensor_tensor(prefix[:, 1:2], prefix[:, 0:1], flips[:, 0:1], ALU.bitwise_xor))
            link(V.tensor_tensor(candidates[:], digits[:, 0], prefix[:, 1:2].to_broadcast([P, 3]), ALU.bitwise_xor))
            ROUNDS = 15
            for r in range(ROUNDS):
                for c in range(3):
                    link(V.tensor_scalar(junk[:, c], keys_flat[:], candidates[:, c:c + 1].bitcast(F32), 0.0,
                                         ALU.is_ge, ALU.add, accum_out=counts[:, c:c + 1]), c == 2)
                V.tensor_copy(counts_bf[:], counts[:]).then_inc(counted, 1)
                dve.wait_ge(summed, 5 + r)
                link(V.tensor_scalar(junk3[:], max_ps[:, 0, 0:3], float(CAP), 0.0, ALU.is_ge, ALU.add,
                                     accum_out=digit[:, 0:1]))
                link(V.tensor_scalar(flips[:, 0:1], digit[:, 0:1], 2.0 ** (2 * (14 - r)), None, ALU.mult))
                old, new = (r + 1) % 2, r % 2
                link(V.tensor_tensor(prefix[:, new:new + 1], prefix[:, old:old + 1], flips[:, 0:1], ALU.bitwise_xor))
                if r + 1 < ROUNDS:
                    link(V.tensor_tensor(candidates[:], digits[:, r + 1], prefix[:, new:new + 1].to_broadcast([P, 3]),
                                         ALU.bitwise_xor))
            threshold = prefix[:, (ROUNDS - 1) % 2:(ROUNDS - 1) % 2 + 1].bitcast(F32)

            link(V.tensor_scalar(above[:], keys_flat[:], threshold, 0.0, ALU.is_gt, ALU.add, accum_out=stats[:, 0:1]), False)
            link(V.tensor_scalar(equal[:], keys_flat[:], threshold, 0.0, ALU.is_equal, ALU.add, accum_out=stats[:, 1:2]), False)
            link(V.tensor_scalar(stats[:, 2:3], threshold, UNASSIGNED / 2, None, ALU.is_gt))
            V.tensor_copy(stats_bf[:, 0:2], stats[:, 0:2]).then_inc(counted, 1)
            dve.wait_ge(summed, 5 + ROUNDS)
            link(V.tensor_scalar(stats[:, 3:4], max_ps[:, 0, 0:1], -1.0, float(CAP), ALU.mult, ALU.add), False)
            link(V.tensor_copy(stats[:, 4:5], max_ps[:, 0, 1:2]))
            link(V.tensor_tensor(stats[:, 5:6], stats[:, 3:4], stats[:, 2:3], ALU.mult), False)
            link(V.tensor_tensor_scan(order_of[:], equal[:], zeros_row[:], stats[:, 4:5], ALU.add, ALU.add))
            link(V.scalar_tensor_tensor(taken[:], order_of[:], stats[:, 5:6], equal[:], ALU.is_le, ALU.mult))
            link(V.scalar_tensor_tensor(taken[:], taken[:], 1.0, above[:], ALU.mult, ALU.add, accum_out=stats[:, 6:7]))
            V.tensor_copy(stats_bf[:, 2:3], stats[:, 6:7]).then_inc(counted, 1)
            dve.wait_ge(summed, 6 + ROUNDS)
            link(V.tensor_copy(stats[:, 7:8], max_ps[:, 0, 0:1]))
            link(V.tensor_tensor_scan(order_of[:], taken[:], zeros_row[:], stats[:, 7:8], ALU.add, ALU.add))
            V.tensor_tensor(slot_flat[:], order_of[:], taken[:], ALU.mult).then_inc(counted, 1)

            dve.wait_ge(gate_pos_ps, 1)
            dve.wait_ge(pool_const, POOL_CONSTS + 6)
            by_pos = bank_b[:, P:2 * P].rearrange("p (t e) -> p t e", t=NT)
            link(V.tensor_copy(token_info[:, :, 0:E, 3], by_pos))
            link(V.tensor_tensor(gate_rest[:, 0], by_pos, token_info[:, :, 0:E, 3], ALU.subtract))
            link(V.tensor_copy(token_info[:, :, 0:E, 4], gate_rest[:, 0]))
            link(V.tensor_tensor(gate_rest[:, 1], gate_rest[:, 0], token_info[:, :, 0:E, 4], ALU.subtract))
            link(V.tensor_copy(token_info[:, :, 0:E, 5], gate_rest[:, 1]))
            dve.wait_ge(slot_pos_ps, 1)
            V.tensor_copy(slot_of[:, :, 0:E], bank_a[:, P:2 * P].rearrange("p (t e) -> p t e", t=NT)).then_inc(slot_pos_ok, 1)
            dve.wait_ge(slot_pos_ok, 1)

            def one_hots(i, par):
                if not isinstance(i, int):
                    dve.wait_ge(p_info, i - 1)
                for t in range(NT):
                    V.tensor_scalar(one_hot[:, par, t], slot_number[:], slot_of[:, t, bass.ds(i, 1)], None,
                                    ALU.is_equal).then_inc(s_hot, 1)

            def rows_of(i, par):
                dve.wait_ge(p_info, i + 1)
                V.tensor_copy(slot_info[:, par], bank_b[:, 0:6 * NM].rearrange("p (m c) -> p m c", c=6)).then_inc(e_info, 1)
                dve.wait_ge(e_info, i + 1)
                info = slot_info[:, par]
                if not isinstance(i, int):
                    dve.wait_ge(scattered, 16 * NM * (i - 1))
                    dve.wait_ge(s_y, NM * (i - 1))
                V.scalar_tensor_tensor(slot_calc[:, par, 0], info[:, :, 0], float(P), info[:, :, 1], ALU.mult, ALU.add).then_inc(s_calc, 1)
                V.tensor_scalar(slot_calc[:, par, 1], info[:, :, 2], -1.0, 1.0, ALU.mult, ALU.add).then_inc(s_calc, 1)
                V.tensor_tensor(slot_calc[:, par, 2], info[:, :, 3], info[:, :, 4], ALU.add).then_inc(s_calc, 1)
                dve.wait_ge(s_calc, 4 * i + 3)
                V.tensor_tensor(slot_calc[:, par, 1], slot_calc[:, par, 1], spare_row[:], ALU.mult).then_inc(s_calc, 1)
                V.tensor_copy(source_row[:, par], slot_calc[:, par, 0])
                V.tensor_tensor(slot_gate[:, par], slot_calc[:, par, 2], info[:, :, 5], ALU.add)
                dve.wait_ge(s_calc, 4 * i + 4)
                V.tensor_tensor(target_row[:, par], slot_calc[:, par, 0], slot_calc[:, par, 1], ALU.add).then_inc(s_rows, 1)

            one_hots(0, 0)
            one_hots(1, 1)
            rows_of(0, 0)
            rows_of(1, 1)
            dve.sem_inc(e_y, NM)
            n_active = dve.value_load(order_i[0:1, E:E + 1], min_val=2, max_val=E)
            with dve.Fori(0, E // 2) as loop:
                for par in range(2):
                    i = 2 * loop + par
                    with dve.If(i + 2 < n_active):
                        one_hots(i + 2, par)
                    with dve.If(i < n_active):
                        for m, (_, rows) in enumerate(SLOTS):
                            dve.wait_ge(p_y, NM * i + m + 1)
                            dve.wait_ge(ld_bias[par], 32 * (loop + 1))
                            if m == 0:
                                dve.wait_ge(s_rows, i + 1)
                            V.tensor_tensor(y_b2[0:rows, m], y_ps[m][0:rows],
                                            b2_bc[0:rows, par], ALU.add).then_inc(e_y, 1)
                            dve.wait_ge(e_y, NM * (i + 1) + m + 1)
                            V.tensor_scalar(y_out[0:rows, par, m], y_b2[0:rows, m], slot_gate[0:rows, par, m:m + 1], None,
                                            ALU.mult).then_inc(s_y, 1)
                    with dve.If(i + 2 < n_active):
                        rows_of(i + 2, par)

            for b in range(B):
                par = b % 2
                dve.wait_ge(ld_acc[b], 16)
                for t in range(T):
                    ins = V.bn_stats(bn3[:, par, t], acc[:, T * b + t])
                ins.then_inc(d_bn, 1)
                dve.wait_ge(d_bn, b + 1)
                for t in range(T):
                    ins = V.bn_aggr(mv3[:, par, t], bn3[:, par, t])
                ins.then_inc(d_mv, 1)
                dve.wait_ge(d_rs, b + 1)
                V.scalar_tensor_tensor(nb3[:, par], mv3[:, par, :, 0], -1.0, rs3[:, par], ALU.mult, ALU.mult).then_inc(d_nb, 1)
                dve.wait_ge(d_gamma, b + 1)
                wait(dve, st_out[par], 16 * (b // 2))
                V.tensor_tensor(result[:, par], scaled[:, par], x2_beta[:, T * b:T * b + T], ALU.add).then_inc(d_res, 1)

        @block.tensor
        def _(pe):
            def mm(out_, lhs, rhs, start=True, stop=True):
                return nc.tensor.matmul(out_, lhs, rhs, start=start, stop=stop, skip_group_check=True)

            def tr(out_, in_, identity):
                return nc.tensor.transpose(out_, in_, identity)

            pe.wait_ge(ld_w[0], 48)
            pe.wait_ge(pool_const, POOL_CONSTS)
            tr(bank_a[:, 0:4], bqk_rows[:, :], ident[0:4, 0:4]).then_inc(bqk_ps, 1)
            pe.wait_ge(act_const, 1)

            def front_ctx(b):
                wait(pe, e_o, 2 * b.n - 2)
                wait(pe, e_ctx, 2 * b.n)
                pe.wait_ge(ld_ctx[b.par], 16 * (b.turn + 1))
                for k in range(KD):
                    tr(bank_b[:, k * SK:(k + 1) * SK], ctx_in[:, b.par, k * P:(k + 1) * P], ident[0:SK, 0:SK])
                pe.wait_ge(s_quarter, b.n + 1)
                for t in range(T):
                    ins = mm(bank_b[:, S + t * P:S + (t + 1) * P], quarter[:, t:t + 1].to_broadcast([P, P]), ident_bf[:])
                ins.then_inc(p_ctx, 1)

            def front_xn(b):
                wait(pe, e_x2, b.n - 1)
                wait(pe, e_kv, 6 * b.n)
                if isinstance(b.n, int) and b.n == 0:
                    pe.wait_ge(bqk_ok, 1)
                pe.wait_ge(s_xn, b.n + 1)
                for k in range(KD):
                    for t in range(T):
                        ins = tr(bank_a[:, k * S + t * P:k * S + (t + 1) * P], xn[:, t, k * P:(k + 1) * P], ident[:])
                ins.then_inc(p_xnt, 1)

            def front_q(b):
                pe.wait_ge(e_xnt, b.n + 1)
                for g in range(G):
                    for k in range(KD):
                        ins = mm(bank_a[:, g * S:(g + 1) * S], wq_sb[:, k, g * P:(g + 1) * P], xn_t[:, k],
                                 start=k == 0, stop=k == KD - 1)
                ins.then_inc(p_q, 1)

            def front_kv(b):
                pe.wait_ge(e_q, G * (b.n + 1))
                wait(pe, e_lg, b.n - 1)
                pe.wait_ge(e_ctx, 2 * (b.n + 1))
                pe.wait_ge(ld_w[1], 16)
                pe.wait_ge(ld_w[2], 32)
                for g in range(G):
                    for k in range(KD):
                        mm(bank_a[:, g * SK:(g + 1) * SK], wk_sb[:, k, g * P:(g + 1) * P], ctx_t[:, k],
                           start=k == 0, stop=k == KD - 1)
                for k in range(KD):
                    ins = mm(bank_a[0:SK, S:2 * S], ctx_t[:, k], wv_sb[:, k], start=k == 0, stop=k == KD - 1)
                ins.then_inc(p_kv, 1)

            def scores_for_max(b, k):
                t, half = k // 2, k % 2
                wait(pe, e_max, 4 * b.n + k)
                if k == 0:
                    wait(pe, e_q, G * (b.n + 1))
                    wait(pe, e_kv, 6 * (b.n + 1))
                    wait(pe, s_mask, T * (b.n + 1))
                for jj in range(2):
                    mm(max_ps[:, jj, 0:4 * SK], ident_bf[:],
                       mask_and_max[:, b.par, t, 0:SK].unsqueeze(1).to_broadcast([P, 4, SK]), stop=False)
                for g in range(G):
                    for jj in range(2):
                        rows = slice(RB * (2 * half + jj), RB * (2 * half + jj + 1))
                        ins = mm(max_ps[:, jj, g * 2 * SK:(g + 1) * 2 * SK], q_t[rows, b.par, g, t * P:(t + 1) * P],
                                 k_t[rows, b.par, g].rearrange("p s k -> p (s k)"), start=False)
                ins.then_inc(p_max, 1)

            def shift_transposed(b):
                wait(pe, e_ctx, 2 * (b.n + 2) if not is_last_batch(b) else 2 * (b.n + 1))
                wait(pe, e_o, 2 * b.n)
                pe.wait_ge(s_lo, b.n + 1)
                for t in range(T):
                    ins = tr(bank_b[:, t * P // 2:(t + 1) * P // 2].bitcast(BF16), mask_and_max[:, b.par, t], ident_bf[:])
                ins.then_inc(p_shift, 1)

            def scores(b, g):
                wait(pe, e_exp, G * b.n + g)
                pe.wait_ge(e_shift, b.n + 1)
                for s in range(2):
                    for j in range(J):
                        mm(score_ps[0:SK, j, s * S:(s + 1) * S], shift_rows[:, head_column(g, j, s)], shift[:],
                           start=s == 0, stop=False)
                for s in range(2):
                    for j in range(J):
                        ins = mm(score_ps[0:SK, j, s * S:(s + 1) * S], k_t[RB * j:RB * (j + 1), b.par, g, s],
                                 q_t[RB * j:RB * (j + 1), b.par, g], start=False)
                ins.then_inc(p_score, 1)

            def weighted_values(b, g):
                if g == 0:
                    pe.wait_ge(e_shift, b.n + 1)
                else:
                    pe.wait_ge(e_o, G * b.n + 1)
                pe.wait_ge(e_exp, G * b.n + g + 1)
                for s in range(2):
                    for j in range(J):
                        mm(bank_b[RB * j:RB * (j + 1), 0:S], v_pad[:, b.par, 8 * g + 2 * j + s], probs[:, g, j, s],
                           start=s == 0, stop=s == 1)
                for s in range(2):
                    for j in range(J):
                        ins = mm(bank_b[RB * j:RB * (j + 1), S:2 * S], half_ones[0:SK, s], probs[:, g, j, s],
                                 start=False, stop=s == 1)
                ins.then_inc(p_pv, 1)

            def back_o(b):
                wait(pe, e_kv, 6 * (b.n + 1) if is_last_batch(b) else 6 * (b.n + 2))
                pe.wait_ge(e_o, G * (b.n + 1))
                pe.wait_ge(ld_w[3], 32)
                for t in range(T):
                    for g in range(G):
                        ins = mm(bank_a[:, t * D:(t + 1) * D], o_t[:, g, t * P:(t + 1) * P], wo_sb[:, g],
                                 start=g == 0, stop=g == G - 1)
                ins.then_inc(p_o, 1)

            def back_z(b):
                if is_last_batch(b):
                    pe.wait_ge(e_x2, b.n + 1)
                elif not is_last_batch(b.plus(1)):
                    pe.wait_ge(e_q, G * (b.n + 3))
                pe.wait_ge(e_z, b.n + 1)
                for k in range(KD):
                    for t in range(T):
                        ins = tr(bank_a[:, k * S + t * P:k * S + (t + 1) * P], z[:, t, k * P:(k + 1) * P], ident[:])
                ins.then_inc(p_zt, 1)

            def back_logits(b):
                pe.wait_ge(e_zt, b.n + 1)
                pe.wait_ge(ld_w[4], 64)
                for t in range(T):
                    for k in range(KD):
                        ins = mm(bank_a[:, t * E:(t + 1) * E], z_t[:, k, t * P:(t + 1) * P], wr_sb[:, k],
                                 start=k == 0, stop=k == KD - 1)
                ins.then_inc(p_lg, 1)

            def is_last_batch(b):
                return isinstance(b.n, int) and b.n == B - 1

            def before(b):
                front_ctx(b)
                front_xn(b)
                front_q(b)
                front_kv(b)

            def body(b, is_first, is_last):
                scores_for_max(b, 0)
                if not is_first:
                    back_o(b.plus(-1))
                scores_for_max(b, 1)
                if not is_last:
                    front_ctx(b.plus(1))
                scores_for_max(b, 2)
                scores_for_max(b, 3)
                if not is_last:
                    front_xn(b.plus(1))
                shift_transposed(b)
                scores(b, 0)
                if not is_last:
                    front_q(b.plus(1))
                if not is_first:
                    back_z(b.plus(-1))
                scores(b, 1)
                if not is_first:
                    back_logits(b.plus(-1))
                weighted_values(b, 0)
                if not is_last:
                    front_kv(b.plus(1))
                weighted_values(b, 1)

            batches(pe, B, before, body)
            last = Batch(0, B - 1)
            back_o(last)
            back_z(last)
            back_logits(last)

            flat = "p t e -> p (t e)"
            pe.wait_ge(keys_ready, 2)
            pe.wait_ge(e_lg, B)
            tr(bank_a[:, 0:P], keys[:].rearrange(flat), ident[:]).then_inc(keys_ps, 1)
            pe.wait_ge(gates_ready, 1)
            pe.wait_ge(e_lg, B)
            tr(bank_b[:, 0:P], gates[:].rearrange(flat), ident[:]).then_inc(gates_ps, 1)
            small = max_ps[:, 0]
            pe.wait_ge(counted, 1)
            mm(small[:, 0:1], same_expert[:], active_bf[:]).then_inc(summed, 1)
            pe.wait_ge(counted, 2)
            mm(small[:, 0:1], earlier_expert[:], active_bf[:])
            mm(small[:, 1:2], same_tile[:], active_bf[:]).then_inc(summed, 1)
            pe.wait_ge(counted, 3)
            mm(small[0:1, 0:E], half_ones[0:E, 0, 0:1], order_rows[:, 0]).then_inc(summed, 1)
            pe.wait_ge(gates_ok, 1)
            mm(bank_b[:, P:2 * P], gates_flat[:], to_position[:]).then_inc(gate_pos_ps, 1)
            for r in range(16):
                pe.wait_ge(counted, 4 + r)
                mm(small[:, 0:3], same_expert[:], counts_bf[:]).then_inc(summed, 1)
            pe.wait_ge(counted, 20)
            mm(small[:, 0:1], same_expert[:], stats_bf[:, 0:1])
            mm(small[:, 1:2], earlier_tile[:], stats_bf[:, 1:2]).then_inc(summed, 1)
            pe.wait_ge(counted, 21)
            mm(small[:, 0:1], earlier_tile[:], stats_bf[:, 2:3]).then_inc(summed, 1)
            pe.wait_ge(counted, 22)
            mm(bank_a[:, P:2 * P], slot_flat[:], to_position[:]).then_inc(slot_pos_ps, 1)

            def slot_map(i, par):
                if not isinstance(i, int) or i > 0:
                    pe.wait_ge(e_info, i)
                for m, (at, rows) in enumerate(SLOTS):
                    for t in range(NT):
                        if m == 0:
                            pe.wait_ge(s_hot, NT * i + t + 1)
                        ins = mm(bank_b[0:rows, 6 * m:6 * m + 6], one_hot[:, par, t, at:at + rows],
                                 token_info[:, t, bass.ds(i, 1)].rearrange("p a c -> p (a c)"), start=t == 0, stop=t == NT - 1)
                ins.then_inc(p_info, 1)

            slot_map(0, 0)
            slot_map(1, 1)
            pe.wait_ge(e_info, 2)
            n_active = pe.value_load(order_i[0:1, E:E + 1], min_val=2, max_val=E)
            with pe.Fori(0, E // 2) as loop:
                for par in range(2):
                    i = 2 * loop + par
                    with pe.If(i < n_active):
                        pe.wait_ge(e_y, NM * (i + 1))
                        pe.wait_ge(ld_bias[par], 32 * (loop + 1))
                        for m in range(NM):
                            pe.wait_ge(gathered[par][m], 16 * (loop + 1))
                        for m, (at, rows) in enumerate(SLOTS):
                            for k, bank in enumerate((bank_a, bank_b)):
                                ins = tr(bank[:, at:at + rows], xe[0:rows, par, m, k * P:(k + 1) * P], ident[0:rows, 0:rows])
                        ins.then_inc(p_xe, 1)
                        tr(max_ps[:, 0, 300:300 + KF], b1_rows[:, par], ident[0:KF, 0:KF]).then_inc(p_b1, 1)
                        pe.wait_ge(ld_w1[par], 16 * (loop + 1))
                        pe.wait_ge(e_xe, 2 * (i + 1))
                        for f in range(KF):
                            if f < J:
                                pass
                            else:
                                pe.wait_ge(e_h, KF * i + f - J + 1)
                            for k in range(KD):
                                ins = mm(score_ps[:, f % J, 0:CAP], w1_sb[:, par, k, f * P:(f + 1) * P], xe_t[:, k],
                                         start=k == 0, stop=k == KD - 1)
                            ins.then_inc(p_h, 1)
                        for m, (at, rows) in enumerate(SLOTS):
                            for f in range(KF):
                                if m == 0:
                                    pe.wait_ge(e_h, KF * i + f + 1)
                                if m == 0 and f == 0:
                                    pe.wait_ge(e_b1, i + 1)
                                    pe.wait_ge(ld_w2[par], 16 * (loop + 1))
                                ins = mm(y_ps[m][0:rows], hidden[:, f, at:at + rows],
                                         w2_sb[:, par, f], start=f == 0, stop=f == KF - 1)
                            ins.then_inc(p_y, 1)
                    with pe.If(i + 2 < n_active):
                        slot_map(i + 2, par)
                        pe.wait_ge(e_info, i + 3)


_INS = ["x", "ctx_1024", "mask_BxSxS2_ik1",
        "L0_xattn_wq_kernel", "L0_xattn_wq_bias", "L0_xattn_wk_kernel", "L0_xattn_wk_bias",
        "L0_xattn_wv_kernel", "L0_xattn_wv_bias", "L0_xattn_wo_kernel", "L0_xattn_wo_bias",
        "L0_ffn_Wr", "L0_ffn_br", "L0_ffn_W1", "L0_ffn_b1", "L0_ffn_W2", "L0_ffn_b2",
        "L0_ffn_gamma", "L0_ffn_beta"]


def kernel(**inputs):
    import numpy as _np
    import concourse.bacc as _bacc
    from concourse import mybir as _mybir
    from concourse.bass_utils import run_bass_kernel_spmd as _run

    nc = _bacc.Bacc("TRN2", target_bir_lowering=False, num_devices=1)
    arrays, args = {}, []
    for name in _INS:
        a = _np.ascontiguousarray(inputs[name])
        arrays[f"in_{name}"] = a
        args.append(nc.dram_tensor(f"in_{name}", a.shape, _mybir.dt.from_np(a.dtype), kind="ExternalInput").ap())
    shape = tuple(inputs["x"].shape)
    args.append(nc.dram_tensor("out_0", shape, _mybir.dt.float32, kind="ExternalOutput").ap())
    xattn_moe(nc, *args)
    r = _run(nc, [arrays], core_ids=[0])
    return r.results[0]["out_0"]
```

```python
from contextlib import ExitStack

import concourse.bass as bass
from concourse import mybir

F32 = mybir.dt.float32
BF16 = mybir.dt.bfloat16
F16 = mybir.dt.float16
I32 = mybir.dt.int32
ALU = mybir.AluOpType
ACT = mybir.ActivationFunctionType
AX = mybir.AxisListType

P = 128
EPS = 1e-5
MASKED = -(2.0 ** 40)
UNASSIGNED = -1000.0
SATURATED = 16.635532
GONE = -110.0


class Batch:

    def __init__(self, loop, offset):
        self.loop, self.offset = loop, offset
        self.n = 2 * loop + offset
        self.par = offset % 2
        self.turn = loop + offset // 2

    def plus(self, k):
        return Batch(self.loop, self.offset + k)


def wait(engine, semaphore, value):
    if isinstance(value, int) and value <= 0:
        return
    engine.wait_ge(semaphore, value)


def batches(engine, count, before, body):
    before(Batch(0, 0))
    body(Batch(0, 0))
    body(Batch(0, 1))
    with engine.Fori(0, (count - 4) // 2) as loop:
        body(Batch(loop, 2))
        body(Batch(loop, 3))
    body(Batch(0, count - 2))
    body(Batch(0, count - 1))


def xattn_moe(nc, x, ctx, mask, wq, bq, wk, bk, wv, bv, wo, bo, wr, br, w1, b1, w2, b2,
              gamma, beta, out):
    B, S, D = x.shape
    SK = ctx.shape[1]
    H = 16
    HD = D // H
    E, _, F = w1.shape
    N = B * S
    CAP = max(-(-N * 5 // (E * 4)), 1)
    T = S // P
    NT = N // P
    KD = D // P
    KF = F // P
    G = D // P
    SLOTS = [(m * P, min(P, CAP - m * P)) for m in range(-(-CAP // P))]
    NM = len(SLOTS)
    RB = 32
    J = P // RB
    NH = 4
    assert T == 2 and G == 2 and HD * 2 == RB and NT * E == P and B % 2 == 0

    z_table = nc.dram_tensor("z_table", (N, D), F32, kind="Internal").ap()
    acc_table = nc.dram_tensor("acc_table", (N + CAP, D), F32, kind="Internal").ap()

    with ExitStack() as stack:
        def sb(name, shape, dt=F32):
            return stack.enter_context(nc.sbuf_tensor(name, shape, dt))

        def ps(name, shape, dt=F32):
            return stack.enter_context(nc.psum_tensor(name, shape, dt))

        def sem(name):
            return stack.enter_context(nc.semaphore(name))

        score_ps = ps("score_ps", [P, 2, 2, 512])
        probs_ps = ps("probs_ps", [P, 2, 512])
        bank_a = ps("bank_a", [P, 512])
        bank_b = ps("bank_b", [P, 512])
        h_ps = score_ps[:].rearrange("p a b c -> p (a b) c")
        small = probs_ps[:, 0]
        small2 = probs_ps[:, 1]
        y_ps = (probs_ps[:, 0, 0:D], probs_ps[:, 1, 0:D], probs_ps[:, 0, D:2 * D])

        wq_sb, wk_sb, wv_sb, wo_sb = (sb(n, [P, KD, D]) for n in ("wq_sb", "wk_sb", "wv_sb", "wo_sb"))
        wr_sb = sb("wr_sb", [P, KD, E])
        bqk_rows = sb("bqk_rows", [4, P])
        bqk = sb("bqk", [P, 4])
        bv_bc, bo_bc, gamma_bc, beta_bc = (sb(n, [P, D]) for n in ("bv_bc", "bo_bc", "gamma_bc", "beta_bc"))
        br_bc = sb("br_bc", [P, E])
        ident = sb("ident", [P, P])
        ident_bf = sb("ident_bf", [P, P], BF16)
        part_i = sb("part_i", [P, 3], I32)
        head_rows = sb("head_rows", [P, P // HD])
        expert_of_p = sb("expert_of_p", [P, 2])
        head_columns = sb("head_columns", [H, G, P])
        ones = sb("ones", [P, 1])
        minus_half = sb("minus_half", [P, 2])
        eps = sb("eps", [P, 2])
        zero_rows = sb("zero_rows", [P, CAP * D // P])

        x_in = sb("x_in", [P, 2, T, D])
        mask_in = sb("mask_in", [P, 2, T, SK], I32)
        ctx_in = sb("ctx_in", [SK, 2, D])
        bn1 = sb("bn1", [P, T, 6])
        mv1 = sb("mv1", [P, T, 2])
        rs1 = sb("rs1", [P, T])
        xn = sb("xn", [P, T, D])
        xn_t = sb("xn_t", [P, KD, S])
        ctx_t = sb("ctx_t", [P, KD, SK])
        valid = sb("valid", [P, T, SK])
        any_valid = sb("any_valid", [P, T])
        quarter = sb("quarter", [P, T], BF16)
        quarter_bc = sb("quarter_bc", [P, S])
        mask_bf = sb("mask_bf", [P, 2, T, SK], BF16)
        q_t = sb("q_t", [P, 2, G, S])
        k_t = sb("k_t", [P, G, SK])
        k_heads = sb("k_heads", [P, 2, H, SK])
        v_pad = sb("v_pad", [SK, 2, H, RB])
        neg_max = sb("neg_max", [P, G, T, 2, 4])
        probs_q = sb("probs_q", [P, G, T, 2, 4, SK])
        probs = sb("probs", [P, 2, J, 2, S])
        denom = sb("denom", [P, T, G, 8])
        recip = sb("recip", [P, T, H])
        recip_t = sb("recip_t", [H, S])
        recip_rows = sb("recip_rows", [P, G, S])
        o_t = sb("o_t", [P, G, S])
        x_bo = sb("x_bo", [P, 2, T, D])
        x2 = sb("x2", [P, T, D])
        x2_beta = sb("x2_beta", [P, NT, D])
        bn2 = sb("bn2", [P, T, 6])
        mv2 = sb("mv2", [P, T, 2])
        rs2 = sb("rs2", [P, T])
        z = sb("z", [P, T, D])
        z_t = sb("z_t", [P, KD, S])
        logits = sb("logits", [P, NT, E])

        rank_weight = sb("rank_weight", [P, NT, E])
        col_expert = sb("col_expert", [P, P])
        col_tile = sb("col_tile", [P, P])
        col_index = sb("col_index", [P, P])
        same_expert = sb("same_expert", [P, P], BF16)
        same_expert_f = sb("same_expert_f", [P, P])
        earlier_tile = sb("earlier_tile", [P, P], BF16)
        same_tile = sb("same_tile", [P, P], BF16)
        earlier_expert = sb("earlier_expert", [P, P], BF16)
        top = sb("top", [P, 2, NT])
        hit = sb("hit", [P, NT, E])
        first = sb("first", [P, NT])
        chosen = sb("chosen", [P, 2, NT, E])
        rest = sb("rest", [P, NT, E])
        gap = sb("gap", [P, NT])
        pair = sb("pair", [P, 3, NT, E])
        keys = sb("keys", [P, NT, E])
        gate_of = sb("gate_of", [P, 4, NT])
        gates = sb("gates", [P, NT, E])
        keys_flat = sb("keys_flat", [P, P])
        gates_flat = sb("gates_flat", [P, P])
        junk = sb("junk", [P, 4, P], BF16)
        junk3 = sb("junk3", [P, 3])
        digits = sb("digits", [P, 15, 3], I32)
        candidates = sb("candidates", [P, 3], I32)
        counts = sb("counts", [P, 3])
        next_prefix = sb("next_prefix", [P, 3], I32)
        digit = sb("digit", [P, 4])
        prefix = sb("prefix", [P, 2], I32)
        flips = sb("flips", [P, 3], I32)
        above = sb("above", [P, P])
        equal = sb("equal", [P, P])
        zeros_row = sb("zeros_row", [P, P])
        order_of = sb("order_of", [P, P])
        taken = sb("taken", [P, P])
        stats = sb("stats", [P, 8])
        stats_bf = sb("stats_bf", [P, 4], BF16)
        slot_flat = sb("slot_flat", [P, P])
        active = sb("active", [P, 8])
        active_bf = sb("active_bf", [P, 1], BF16)
        to_position = sb("to_position", [P, P])
        order_rows = sb("order_rows", [E, 2, E])
        order_i = sb("order_i", [1, E + 1], I32)
        slot_of = sb("slot_of", [P, NT, E + 2])
        gate_rest = sb("gate_rest", [P, 2, NT, E])

        slot_number = sb("slot_number", [P, CAP], F16)
        token_info = sb("token_info", [P, NT, E + 2, 6], BF16)
        one_hot = sb("one_hot", [P, 2, NT, CAP], BF16)
        spare_row = sb("spare_row", [P, NM])
        slot_info = sb("slot_info", [P, 2, NM, 6])
        slot_calc = sb("slot_calc", [P, 2, 3, NM])
        slot_gate = sb("slot_gate", [P, 2, NM])
        source_row = sb("source_row", [P, 2, NM], I32)
        target_row = sb("target_row", [P, 2, NM], I32)
        w1_sb = sb("w1_sb", [P, 2, KD, F])
        w2_sb = sb("w2_sb", [P, 2, KF, D])
        b1_rows = sb("b1_rows", [KF, 2, P])
        b1_t = sb("b1_t", [P, 2, KF])
        b2_bc = sb("b2_bc", [P, 2, D])
        xe = sb("xe", [P, 2, NM, D])
        xe_t = sb("xe_t", [P, KD, CAP])
        hidden = probs[:].rearrange("p a j s q -> p (a j s q)")[:, 0:KF * CAP].rearrange(
            "p (f c) -> p f c", c=CAP)
        y_b2 = sb("y_b2", [P, NM, D])
        y_out = sb("y_out", [P, 2, NM, D])

        acc = w1_sb[:].rearrange("p a k f -> p (a k f)").rearrange("p (t d) -> p t d", d=D)
        scaled = w2_sb[:].rearrange("p a k d -> p (a k d)").rearrange("p (t d) -> p t d", d=D)
        bn3 = sb("bn3", [P, NT, 6])
        mv3 = sb("mv3", [P, NT, 2])
        rs3 = sb("rs3", [P, NT])
        nb3 = sb("nb3", [P, NT])

        ld_wq = sem("ld_wq")
        ld_w = [sem(f"ld_w{k}") for k in range(5)]
        ld_x, ld_mask, ld_ctx = ([sem(f"{n}{p}") for p in range(2)] for n in ("ld_x", "ld_mask", "ld_ctx"))
        ld_bias, ld_w1, ld_w2 = ([sem(f"{n}{p}") for p in range(2)] for n in ("ld_bias", "ld_w1", "ld_w2"))
        ld_acc = [sem(f"ld_acc{p}") for p in range(B)]
        st_z, st_zero, st_out = sem("st_z"), sem("st_zero"), sem("st_out")
        pool_const, dve_const, act_const = sem("pool_const"), sem("dve_const"), sem("act_const")
        bqk_ps, bqk_ok = sem("bqk_ps"), sem("bqk_ok")
        s_bn1, s_mv1, s_add1, s_rs1, s_xn, s_xbo = (sem(n) for n in ("bn1_ok", "mv1_ok", "add1_ok", "rs1_ok", "xn_ok", "xbo_ok"))
        s_valid, s_mask, s_quarter, s_heads = (sem(n) for n in ("valid_ok", "mask_ok", "quarter_ok", "k_heads_ok"))
        p_ctx, e_ctx, p_xnt, e_xnt, p_q, e_q, p_kv, e_kv = (sem(n) for n in (
            "ctx_t_ps", "ctx_t_ok", "xn_t_ps", "xn_t_ok", "q_ps", "q_ok", "kv_ps", "kv_ok"))
        p_scores, s_max, s_sub, e_exp, s_denom, s_recip = (sem(n) for n in (
            "scores_ok", "max_ok", "shifted_ok", "exp_ok", "denom_ok", "recip_ok"))
        p_probs, e_probs, p_recip, e_recip, p_rows, e_rows, p_pv, e_o = (sem(n) for n in (
            "probs_t_ps", "probs_ok", "recip_t_ps", "recip_t_ok", "recip_rows_ps", "recip_rows_ok", "pv_ps", "o_t_ok"))
        p_o, e_x2, s_bn2, s_mv2, s_add2, s_rs2, s_x2b, e_z, p_zt, e_zt, p_lg, e_lg = (sem(n) for n in (
            "o_ps", "x2_ok", "bn2_ok", "mv2_ok", "add2_ok", "rs2_ok", "x2_beta_ok", "z_ok", "z_t_ps",
            "z_t_ok", "logits_ps", "logits_ok"))
        dve_b = sem("dve_b")
        keys_ready, keys_ps, keys_ok, e_ok, gates_ready, gates_ps, gates_ok = (sem(n) for n in (
            "keys_ready", "keys_ps", "keys_ok", "exp_gap_ok", "gates_ready", "gates_ps", "gates_ok"))
        counted, summed = sem("counted"), sem("summed")
        active_step, active_sum = sem("active_step"), sem("active_sum")
        order_ready = sem("order_ready")
        gate_pos_ps, slot_pos_ps, slot_pos_ok = (sem(n) for n in (
            "gate_pos_ps", "slot_pos_ps", "slot_pos_ok"))
        s_hot, p_info, e_info, s_calc, s_rows = (sem(n) for n in (
            "one_hot_ok", "slot_info_ps", "slot_info_ok", "slot_calc_ok", "rows_ok"))
        gathered = [[sem(f"gathered{p}_{m}") for m in range(NM)] for p in range(2)]
        p_xe, e_xe, p_h, e_h, p_y, e_y, s_y, scattered = (sem(n) for n in (
            "xe_t_ps", "xe_t_ok", "h_ps", "h_ok", "y_ps", "y_b2_ok", "y_ok", "scattered"))
        experts_done = sem("experts_done")
        d_bn, d_mv, d_add, d_rs, d_nb, d_norm, d_gamma, d_res = (sem(n) for n in (
            "d_bn", "d_mv", "d_add", "d_rs", "d_nb", "d_norm", "d_gamma", "d_res"))
        d_own_gamma = sem("d_own_gamma")
        OWN = (1, 3, 5)
        SHARED = (0, 2, 4, 6, 7)
        FINISHED = (1, 3, 0, 5, 2, 4, 6, 7)
        assert B == 8

        FIRST_CONSTS, POOL_CONSTS = 9, 18
        x_by_tile = x.rearrange("b (t p) d -> b p t d", p=P)
        out_by_tile = out.rearrange("b (t p) d -> b p t d", p=P)
        mask_by_tile = mask.rearrange("b (t p) k -> b p t k", p=P)
        z_rows = z_table.rearrange("(b t p) d -> b p t d", t=T, p=P)
        acc_rows = acc_table[0:N].rearrange("(b t p) d -> b p t d", t=T, p=P)
        spare_rows = acc_table[N:N + CAP].rearrange("r d -> (r d)").rearrange("(p c) -> p c", p=P)

        def exists(b):
            return not isinstance(b.n, int) or 0 <= b.n < B

        block = stack.enter_context(nc.Block())

        @block.sync
        def _(sp):
            def load_batch(b):
                wait(sp, s_xbo, b.n - 1)
                wait(sp, s_xn, b.n - 1)
                sp.dma_start(x_in[:, b.par], x_by_tile[b.n]).then_inc(ld_x[b.par], 16)
                wait(sp, s_valid, b.n - 1)
                sp.dma_start(mask_in[:, b.par], mask_by_tile[b.n]).then_inc(ld_mask[b.par], 16)
                wait(sp, p_ctx, b.n - 1)
                sp.dma_start(ctx_in[:, b.par], ctx[b.n]).then_inc(ld_ctx[b.par], 16)

            def store_z(b):
                wait(sp, e_z, b.n + 1)
                sp.dma_start(z_rows[b.n], z[:]).then_inc(st_z, 16)
                sp.dma_start(acc_rows[b.n], z[:]).then_inc(st_z, 16)

            def before(b):
                sp.dma_start(bqk_rows[0:2], bq.rearrange("(g p) -> g p", p=P)).then_inc(ld_w[0], 16)
                sp.dma_start(bqk_rows[2:4], bk.rearrange("(g p) -> g p", p=P)).then_inc(ld_w[0], 16)
                load_batch(b)
                sp.dma_start(wk_sb[:], wk.rearrange("(k p) n -> p k n", p=P)).then_inc(ld_w[1], 16)
                sp.dma_start(wv_sb[:], wv.rearrange("(k p) n -> p k n", p=P)).then_inc(ld_w[2], 16)
                sp.dma_start(bv_bc[:], bv.partition_broadcast(P)).then_inc(ld_w[2], 16)
                sp.dma_start(wq_sb[:], wq.rearrange("(k p) n -> p k n", p=P)).then_inc(ld_wq, 16)
                load_batch(b.plus(1))
                sp.dma_start(wo_sb[:], wo.rearrange("(k p) n -> p k n", p=P)).then_inc(ld_w[3], 16)
                sp.dma_start(bo_bc[:], bo.partition_broadcast(P)).then_inc(ld_w[3], 16)
                sp.dma_start(wr_sb[:], wr.rearrange("(k p) n -> p k n", p=P)).then_inc(ld_w[4], 16)
                sp.dma_start(br_bc[:], br.partition_broadcast(P)).then_inc(ld_w[4], 16)
                sp.dma_start(gamma_bc[:], gamma.partition_broadcast(P)).then_inc(ld_w[4], 16)
                sp.dma_start(beta_bc[:], beta.partition_broadcast(P)).then_inc(ld_w[4], 16)
                wait(sp, pool_const, POOL_CONSTS)
                sp.dma_start(spare_rows, zero_rows[:]).then_inc(st_zero, 16)

            def body(b):
                if exists(b.plus(2)):
                    load_batch(b.plus(2))
                if exists(b.plus(-1)):
                    store_z(b.plus(-1))

            batches(sp, B, before, body)
            store_z(Batch(0, B - 1))

            sp.wait_ge(order_ready, 1)
            n_active = sp.value_load(order_i[0:1, E:E + 1], min_val=2, max_val=E)

            def load_expert(i, par):
                e = sp.value_load(order_i[0:1, bass.ds(i, 1)], min_val=0, max_val=E - 1)
                of = bass.ds(e, 1)
                sp.dma_start(b1_rows[:, par], b1[of].rearrange("e (k p) -> k (e p)", p=P)).then_inc(ld_bias[par], 16)
                sp.dma_start(b2_bc[:, par], b2[of].partition_broadcast(P).rearrange("p e d -> p (e d)")).then_inc(ld_bias[par], 16)
                sp.dma_start(w1_sb[:, par], w1[of].rearrange("e (k p) f -> p (e k) f", p=P)).then_inc(ld_w1[par], 16)
                sp.dma_start(w2_sb[:, par], w2[of].rearrange("e (k p) d -> p (e k) d", p=P)).then_inc(ld_w2[par], 16)

            load_expert(0, 0)
            load_expert(1, 1)
            with sp.Fori(0, (E - 2) // 2) as loop:
                for par in range(2):
                    i = 2 * loop + par
                    with sp.If(i + 2 < n_active):
                        sp.wait_ge(s_y, NM * (i + 1))
                        load_expert(i + 2, par)

            sp.wait_ge(experts_done, 1)
            for b in range(B):
                sp.dma_start(acc[:, T * b:T * b + T], acc_rows[b]).then_inc(ld_acc[b], 16)

            def store_out(b):
                sp.dma_start(out_by_tile[b], acc[:, T * b:T * b + T]).then_inc(st_out, 16)

            for n, b in enumerate(FINISHED):
                sp.wait_ge(d_res, n + 1)
                store_out(b)
            sp.wait_ge(st_out, 16 * B)

        @block.gpsimd
        def _(pool):
            made = [0]

            def const(ins, then=False):
                ins.then_inc(pool_const, 1)
                made[0] += 1
                if then:
                    pool.wait_ge(pool_const, made[0])

            imprecise = dict(allow_small_or_imprecise_dtypes=True)
            const(nc.gpsimd.memset(ident[:], 0.0), True)
            const(nc.gpsimd.affine_select(out=ident[:], in_=ident[:], compare_op=ALU.not_equal, fill=1.0,
                                          base=0, pattern=[[-1, P]], channel_multiplier=1))
            const(nc.gpsimd.iota(part_i[:, 0:1], pattern=[[0, 1]], base=0, channel_multiplier=1))
            const(nc.gpsimd.memset(minus_half[:], -0.5))
            const(nc.gpsimd.memset(eps[:], EPS))
            const(nc.gpsimd.memset(v_pad[:], 0.0))
            const(nc.gpsimd.memset(head_rows[:], 1.0), True)
            const(nc.gpsimd.affine_select(out=head_rows[:], in_=head_rows[:], compare_op=ALU.is_ge, fill=0.0,
                                          base=0, pattern=[[-HD, P // HD]], channel_multiplier=1), True)
            const(nc.gpsimd.affine_select(out=head_rows[:], in_=head_rows[:], compare_op=ALU.is_ge, fill=0.0,
                                          base=HD - 1, pattern=[[HD, P // HD]], channel_multiplier=-1))
            assert made[0] == FIRST_CONSTS

            def later_constants():
                const(nc.gpsimd.memset(ones[:], 1.0))
                const(nc.gpsimd.memset(head_columns[:], 1.0), True)
                const(nc.gpsimd.affine_select(out=head_columns[:], in_=head_columns[:], compare_op=ALU.is_ge, fill=0.0,
                                              base=0, pattern=[[P, G], [1, P]], channel_multiplier=-HD), True)
                const(nc.gpsimd.affine_select(out=head_columns[:], in_=head_columns[:], compare_op=ALU.is_ge, fill=0.0,
                                              base=HD - 1, pattern=[[-P, G], [-1, P]], channel_multiplier=HD))
                const(nc.gpsimd.memset(zero_rows[:], 0.0))
                const(nc.gpsimd.iota(col_expert[:], pattern=[[0, NT], [1, E]], base=0, channel_multiplier=0, **imprecise))
                const(nc.gpsimd.iota(col_tile[:], pattern=[[1, NT], [0, E]], base=0, channel_multiplier=0, **imprecise))
                const(nc.gpsimd.iota(col_index[:], pattern=[[1, P]], base=0, channel_multiplier=0, **imprecise))
                const(nc.gpsimd.iota(rank_weight[:], pattern=[[0, NT], [-1, E]], base=E, channel_multiplier=0, **imprecise))
                assert made[0] == POOL_CONSTS

            def scale_of(mv, rs, have_mv, added, have_rs, count):
                wait(pool, have_mv, count)
                nc.gpsimd.tensor_tensor(rs[:], mv[:, :, 1], eps[:], ALU.add).then_inc(added, 1)
                wait(pool, added, count)
                nc.gpsimd.tensor_tensor(rs[:], rs[:], minus_half[:], ALU.pow).then_inc(have_rs, 1)

            def front(b):
                wait(pool, s_xn, b.n)
                scale_of(mv1, rs1, s_mv1, s_add1, s_rs1, b.n + 1)

            def residual_input(b):
                pool.wait_ge(ld_w[3], 32)
                wait(pool, e_x2, b.n - 1)
                pool.wait_ge(ld_x[b.par], 16 * (b.turn + 1))
                nc.gpsimd.tensor_tensor(x_bo[:, b.par], x_in[:, b.par],
                                        bo_bc[:].unsqueeze(1).to_broadcast([P, T, D]), ALU.add).then_inc(s_xbo, 1)

            def front_k(b):
                pool.wait_ge(e_kv, 4 * b.n + 2)
                wait(pool, p_scores, 4 * (b.n - 1))
                for g in range(G):
                    ins = nc.gpsimd.tensor_tensor(
                        k_heads[:, b.par, g * (H // G):(g + 1) * (H // G)],
                        k_t[:, g].unsqueeze(1).to_broadcast([P, H // G, SK]),
                        head_rows[:].unsqueeze(2).to_broadcast([P, H // G, SK]), ALU.mult)
                ins.then_inc(s_heads, 1)

            def back_scale(b):
                wait(pool, e_z, b.n)
                scale_of(mv2, rs2, s_mv2, s_add2, s_rs2, b.n + 1)

            def back(b):
                pool.wait_ge(ld_w[4], 64)
                nc.gpsimd.tensor_tensor(x2_beta[:, bass.ds(T * b.n, T)], x2[:],
                                        beta_bc[:].unsqueeze(1).to_broadcast([P, T, D]), ALU.add).then_inc(s_x2b, 1)

            def before(b):
                front(b)
                front_k(b)
                front(b.plus(1))
                later_constants()
                residual_input(b)

            def body(b):
                if exists(b.plus(-1)):
                    back_scale(b.plus(-1))
                if exists(b.plus(1)):
                    front_k(b.plus(1))
                    residual_input(b.plus(1))
                if exists(b.plus(-1)):
                    back(b.plus(-1))
                if exists(b.plus(2)):
                    front(b.plus(2))

            batches(pool, B, before, body)
            back_scale(Batch(0, B - 1))
            back(Batch(0, B - 1))

            nc.gpsimd.iota(slot_number[:], pattern=[[1, CAP]], base=1, channel_multiplier=0, **imprecise).then_inc(pool_const, 1)
            nc.gpsimd.iota(token_info[:, :, :, 0], pattern=[[1, NT], [0, E + 2]], base=0, channel_multiplier=0, **imprecise).then_inc(pool_const, 1)
            nc.gpsimd.iota(token_info[:, :, :, 1], pattern=[[0, NT], [0, E + 2]], base=0, channel_multiplier=1, **imprecise).then_inc(pool_const, 1)
            nc.gpsimd.memset(token_info[:, :, :, 2:6], 1.0).then_inc(pool_const, 1)
            nc.gpsimd.iota(spare_row[:], pattern=[[P, NM]], base=N, channel_multiplier=1, **imprecise).then_inc(pool_const, 1)
            nc.gpsimd.memset(slot_of[:], 0.0).then_inc(pool_const, 1)

            last_z_row, last_acc_row = pool.to_reg(N - 1), pool.to_reg(N + CAP - 1)

            def gather(i, par):
                pool.wait_ge(s_rows, i + 1)
                for m, (_, rows) in enumerate(SLOTS):
                    nc.gpsimd.indirect_dma_start(
                        xe[0:rows, par, m], None, z_table,
                        bass.IndirectOffsetOnAxis(ap=source_row[0:rows, par, m:m + 1], axis=0),
                        bounds_check=last_z_row, oob_is_err=False).then_inc(gathered[par][m], 16)

            pool.wait_ge(st_z, 32 * B)
            pool.wait_ge(st_zero, 16)
            gather(0, 0)
            gather(1, 1)
            pool.wait_ge(order_ready, 1)
            n_active = pool.value_load(order_i[0:1, E:E + 1], min_val=2, max_val=E)

            def add_rows(i, par):
                if i > 0:
                    pool.wait_ge(scattered, 16 * NM * i)
                for m, (_, rows) in enumerate(SLOTS):
                    pool.wait_ge(s_y, NM * i + m + 1)
                    nc.gpsimd.indirect_dma_start(
                        acc_table, bass.IndirectOffsetOnAxis(ap=target_row[0:rows, par, m:m + 1], axis=0),
                        y_out[0:rows, par, m], None, bounds_check=last_acc_row, oob_is_err=True,
                        compute_op=ALU.add).then_inc(scattered, 16)

            def position(i):
                add_rows(i, i % 2)
                if i + 2 < E:
                    with pool.If(i + 2 < n_active):
                        pool.wait_ge(p_xe, i + 1)
                        gather(i + 2, i % 2)

            def positions_from(i):
                with pool.If(i < n_active):
                    position(i)
                    pool.wait_ge(scattered, 16 * NM * (i + 1))
                    if i + 1 < E:
                        positions_from(i + 1)

            position(0)
            position(1)
            pool.wait_ge(scattered, 16 * NM * 2)
            positions_from(2)
            nc.gpsimd.memset(junk3[:], 0.0).then_inc(experts_done, 1)

            def scale_pair(c):
                tiles = slice(2 * T * c, 2 * T * (c + 1))
                pool.wait_ge(d_mv, c + 1)
                nc.gpsimd.tensor_tensor(rs3[:, tiles], mv3[:, tiles, 1], eps[:, 0:1].to_broadcast([P, 2 * T]), ALU.add).then_inc(d_add, 1)
                pool.wait_ge(d_add, c + 1)
                nc.gpsimd.tensor_tensor(rs3[:, tiles], rs3[:, tiles], minus_half[:, 0:1].to_broadcast([P, 2 * T]), ALU.pow).then_inc(d_rs, 1)

            def times_gamma(b):
                pool.wait_ge(d_norm, b + 1)
                nc.gpsimd.tensor_tensor(scaled[:, T * b:T * b + T], acc[:, T * b:T * b + T],
                                        gamma_bc[:].unsqueeze(1).to_broadcast([P, T, D]), ALU.mult).then_inc(d_gamma, 1)

            scale_pair(0)
            scale_pair(1)
            times_gamma(SHARED[0])
            scale_pair(2)
            scale_pair(3)
            for b in SHARED[1:]:
                times_gamma(b)

        @block.scalar
        def _(act):
            act.wait_ge(pool_const, FIRST_CONSTS)
            nc.scalar.copy(ident_bf[:], ident[:]).then_inc(act_const, 1)
            act.wait_ge(bqk_ps, 1)
            nc.scalar.copy(bqk[:], bank_a[:, 0:4]).then_inc(bqk_ok, 1)

            def ctx_and_quarter(b):
                wait(act, p_kv, b.n)
                wait(act, e_q, 2 * b.n)
                act.wait_ge(p_ctx, b.n + 1)
                nc.scalar.copy(ctx_t[:], bank_b[:, 0:KD * SK].rearrange("p (k c) -> p k c", k=KD)).then_inc(e_ctx, 1)
                nc.scalar.copy(quarter_bc[:], bank_b[:, S:2 * S]).then_inc(e_ctx, 1)

            def xn_transposed(b):
                wait(act, p_q, b.n)
                act.wait_ge(p_xnt, b.n + 1)
                nc.scalar.copy(xn_t[:].rearrange("p k s -> p (k s)"), bank_a[:]).then_inc(e_xnt, 1)

            def exponential(b, k):
                g, t = k // T, k % T
                act.wait_ge(s_sub, 4 * b.n + k + 1)
                piece = probs_q[:, g, t].rearrange("p a c k -> p (a c k)")
                nc.scalar.activation(piece, piece, ACT.Exp).then_inc(e_exp, 1)

            def probs_transposed(b, g, j):
                act.wait_ge(p_probs, H // 2 * b.n + J * g + j + 1)
                if j == 0:
                    wait(act, p_pv, G * (b.n - 1) + g + 1)
                nc.scalar.copy(probs[0:SK, g, j].rearrange("k s q -> k (s q)"), probs_ps[0:SK, j % 2]).then_inc(e_probs, 1)

            def recip_transposed(b):
                wait(act, p_rows, b.n)
                act.wait_ge(p_recip, b.n + 1)
                nc.scalar.copy(recip_t[:], bank_b[0:H, 0:S]).then_inc(e_recip, 1)

            def recip_by_row(b):
                wait(act, e_o, G * b.n)
                act.wait_ge(p_rows, b.n + 1)
                nc.scalar.copy(recip_rows[:].rearrange("p g s -> p (g s)"), bank_b[:]).then_inc(e_rows, 1)

            def z_transposed(b):
                wait(act, p_lg, b.n)
                act.wait_ge(p_zt, b.n + 1)
                nc.scalar.copy(z_t[:].rearrange("p k s -> p (k s)"), bank_a[:]).then_inc(e_zt, 1)

            def body(b):
                exponential(b, 0)
                exponential(b, 1)
                exponential(b, 2)
                if exists(b.plus(1)):
                    ctx_and_quarter(b.plus(1))
                    xn_transposed(b.plus(1))
                probs_transposed(b, 0, 0)
                probs_transposed(b, 0, 1)
                probs_transposed(b, 0, 2)
                exponential(b, 3)
                probs_transposed(b, 0, 3)
                probs_transposed(b, 1, 0)
                probs_transposed(b, 1, 1)
                recip_transposed(b)
                recip_by_row(b)
                probs_transposed(b, 1, 2)
                if exists(b.plus(-1)):
                    z_transposed(b.plus(-1))
                probs_transposed(b, 1, 3)

            def before(b):
                ctx_and_quarter(b)
                xn_transposed(b)

            batches(act, B, before, body)
            z_transposed(Batch(0, B - 1))

            act.wait_ge(keys_ready, 1)
            nc.scalar.activation(gate_of[:, 0], gap[:], ACT.Exp, scale=-1.0).then_inc(e_ok, 1)
            act.wait_ge(keys_ps, 1)
            nc.scalar.copy(keys_flat[:], bank_a[:, 0:P]).then_inc(keys_ok, 1)
            act.wait_ge(gates_ps, 1)
            nc.scalar.copy(gates_flat[:], bank_b[:, 0:P]).then_inc(gates_ok, 1)

            act.wait_ge(order_ready, 1)
            n_active = act.value_load(order_i[0:1, E:E + 1], min_val=2, max_val=E)

            def rows_transposed(i, par):
                act.wait_ge(p_xe, i + 1)
                nc.scalar.copy(xe_t[:, 0], bank_a[:, 0:CAP]).then_inc(e_xe, 1)
                nc.scalar.copy(xe_t[:, 1], bank_b[:, 0:CAP]).then_inc(e_xe, 1)
                nc.scalar.copy(b1_t[:, par], bank_a[:, CAP:CAP + KF]).then_inc(e_xe, 1)

            rows_transposed(0, 0)
            with act.Fori(0, E // 2) as loop:
                for par in range(2):
                    i = 2 * loop + par
                    with act.If(i < n_active):
                        act.wait_ge(e_xe, 3 * (i + 1))
                        for k in range(KF):
                            act.wait_ge(p_h, KF * i + k + 1)
                            nc.scalar.activation(hidden[:, k], h_ps[:, k % NH, 0:CAP], ACT.Gelu,
                                                 bias=b1_t[:, par, k:k + 1]).then_inc(e_h, 1)
                    with act.If(i + 1 < n_active):
                        rows_transposed(i + 1, 1 - par)

            for b in range(B):
                act.wait_ge(d_nb, b // 2 + 1)
                for t in range(T * b, T * b + T):
                    ins = nc.scalar.activation(acc[:, t], acc[:, t], ACT.Identity, bias=nb3[:, t:t + 1],
                                               scale=rs3[:, t:t + 1])
                ins.then_inc(d_norm, 1)

        @block.vector
        def _(dve):
            V = nc.vector
            dve.wait_ge(pool_const, FIRST_CONSTS)
            made = [0]

            def const(ins, then=False):
                ins.then_inc(dve_const, 1)
                made[0] += 1
                if then:
                    dve.wait_ge(dve_const, made[0])

            const(V.tensor_scalar(part_i[:, 1:2], part_i[:, 0:1], E - 1, None, ALU.bitwise_and))
            const(V.tensor_scalar(part_i[:, 2:3], part_i[:, 0:1], 3, None, ALU.logical_shift_right), True)
            const(V.tensor_copy(expert_of_p[:], part_i[:, 1:3]), True)

            def front_a(b):
                dve.wait_ge(ld_x[b.par], 16 * (b.turn + 1))
                for t in range(T):
                    V.bn_stats(bn1[:, t], x_in[:, b.par, t]).then_inc(s_bn1, 1)
                dve.wait_ge(ld_mask[b.par], 16 * (b.turn + 1))
                wait(dve, s_rs1, b.n)
                wait(dve, s_xn, b.n)
                dve.wait_ge(s_bn1, T * (b.n + 1))
                for t in range(T):
                    ins = V.tensor_scalar(valid[:, t], mask_in[:, b.par, t], 0.0, 0.0, ALU.not_equal, ALU.max,
                                          accum_out=any_valid[:, t:t + 1])
                ins.then_inc(s_valid, 1)
                for t in range(T):
                    ins = V.bn_aggr(mv1[:, t], bn1[:, t])
                ins.then_inc(s_mv1, 1)
                wait(dve, p_scores, 4 * (b.n - 1))
                dve.wait_ge(s_valid, b.n + 1)
                wait(dve, p_ctx, b.n)
                for t in range(T):
                    V.tensor_scalar(mask_bf[:, b.par, t], valid[:, t], any_valid[:, t:t + 1], -MASKED,
                                    ALU.subtract, ALU.mult).then_inc(s_mask, 1)
                V.tensor_scalar(quarter[:], any_valid[:], float(HD) ** -0.5, None, ALU.mult).then_inc(s_quarter, 1)

            def front_xn(b):
                dve.wait_ge(s_rs1, b.n + 1)
                wait(dve, p_xnt, b.n)
                for t in range(T):
                    ins = V.tensor_scalar(xn[:, t], x_in[:, b.par, t], mv1[:, t, 0:1], rs1[:, t:t + 1],
                                          ALU.subtract, ALU.mult)
                ins.then_inc(s_xn, 1)

            def front_q(b):
                dve.wait_ge(p_q, b.n + 1)
                dve.wait_ge(e_ctx, 2 * (b.n + 1))
                for g in range(G):
                    V.scalar_tensor_tensor(q_t[:, b.par, g], bank_a[:, g * S:(g + 1) * S], bqk[:, g:g + 1],
                                           quarter_bc[:], ALU.add, ALU.mult).then_inc(e_q, 1)

            def front_kv(b):
                dve.wait_ge(p_kv, b.n + 1)
                wait(dve, s_heads, b.n)
                wait(dve, p_pv, G * (b.n - 1))
                for g in range(G):
                    V.tensor_scalar(k_t[:, g], bank_a[:, g * SK:(g + 1) * SK], bqk[:, 2 + g:3 + g], None,
                                    ALU.add).then_inc(e_kv, 1)
                for s in range(2):
                    V.tensor_tensor(
                        v_pad[:, b.par].rearrange("k (h s) c -> k h s c", s=2)[:, :, s, s * HD:(s + 1) * HD],
                        bank_a[0:SK, S:2 * S].rearrange("k (h s c) -> k h s c", s=2, c=HD)[:, :, s],
                        bv_bc[0:SK].rearrange("k (h s c) -> k h s c", s=2, c=HD)[:, :, s], ALU.add).then_inc(e_kv, 1)

            def shift_scores(b, k):
                g, t = k // T, k % T
                by_head = score_ps[:, k % 2, :, 0:4 * SK].rearrange("p j (c k) -> p j c k", k=SK)
                dve.wait_ge(p_scores, 4 * b.n + k + 1)
                if k == 0:
                    wait(dve, s_sub, 4 * b.n)
                V.tensor_reduce(neg_max[:, g, t], by_head, AX.X, ALU.max, negate=True).then_inc(s_max, 1)
                if k == 0:
                    wait(dve, p_probs, H // 2 * b.n)
                    wait(dve, s_denom, 4 * b.n)
                dve.wait_ge(s_max, 4 * b.n + k + 1)
                V.tensor_tensor(probs_q[:, g, t], by_head, neg_max[:, g, t].unsqueeze(3).to_broadcast([P, 2, 4, SK]),
                                ALU.add).then_inc(s_sub, 1)

            def sum_of(b, k):
                g, t = k // T, k % T
                dve.wait_ge(e_exp, 4 * b.n + k + 1)
                if k == 0:
                    wait(dve, s_recip, b.n)
                V.tensor_reduce(denom[:, t, g], probs_q[:, g, t].rearrange("p a c k -> p (a c) k"), AX.X, ALU.add).then_inc(s_denom, 1)

            def reciprocals(b):
                dve.wait_ge(s_denom, 4 * (b.n + 1))
                wait(dve, p_recip, b.n)
                V.reciprocal(recip[:], denom[:].rearrange("p t g h -> p t (g h)")).then_inc(s_recip, 1)

            def normalise(b, g):
                dve.wait_ge(p_pv, G * b.n + g + 1)
                if g == 0:
                    wait(dve, p_o, b.n)
                dve.wait_ge(e_rows, b.n + 1)
                V.tensor_tensor(o_t[:, g], bank_b[:, g * S:(g + 1) * S], recip_rows[:, g], ALU.mult).then_inc(e_o, 1)

            def back_x2(b):
                dve.wait_ge(p_o, b.n + 1)
                dve.wait_ge(s_xbo, b.n + 1)
                wait(dve, s_x2b, b.n)
                wait(dve, e_z, b.n)
                V.tensor_tensor(x2[:], bank_a[:].rearrange("p (t d) -> p t d", t=T), x_bo[:, b.par], ALU.add).then_inc(e_x2, 1)

            def back_bn(b):
                dve.wait_ge(e_x2, b.n + 1)
                for t in range(T):
                    ins = V.bn_stats(bn2[:, t], x2[:, t])
                ins.then_inc(s_bn2, 1)
                dve.wait_ge(s_bn2, b.n + 1)
                wait(dve, s_rs2, b.n)

            def back_mv(b):
                for t in range(T):
                    ins = V.bn_aggr(mv2[:, t], bn2[:, t])
                ins.then_inc(s_mv2, 1)

            def back_z(b):
                dve.wait_ge(s_rs2, b.n + 1)
                wait(dve, p_zt, b.n)
                wait(dve, st_z, 32 * b.n)
                for t in range(T):
                    ins = V.tensor_scalar(z[:, t], x2[:, t], mv2[:, t, 0:1], rs2[:, t:t + 1], ALU.subtract, ALU.mult)
                ins.then_inc(e_z, 1)

            def back_logits(b):
                dve.wait_ge(ld_w[4], 64)
                dve.wait_ge(p_lg, b.n + 1)
                V.tensor_tensor(logits[:, bass.ds(T * b.n, T)], bank_a[:, 0:T * E].rearrange("p (t e) -> p t e", t=T),
                                br_bc[:].unsqueeze(1).to_broadcast([P, T, E]), ALU.add).then_inc(e_lg, 1)

            def before(b):
                front_a(b)
                dve.wait_ge(bqk_ok, 1)
                dve.wait_ge(ld_w[2], 32)
                front_xn(b)
                front_kv(b)
                front_q(b)
                front_a(b.plus(1))

            def body(b):
                if exists(b.plus(1)):
                    front_xn(b.plus(1))
                shift_scores(b, 0)
                if exists(b.plus(-1)):
                    normalise(b.plus(-1), 1)
                shift_scores(b, 1)
                shift_scores(b, 2)
                if exists(b.plus(-1)):
                    back_x2(b.plus(-1))
                shift_scores(b, 3)
                if exists(b.plus(-1)):
                    back_bn(b.plus(-1))
                sum_of(b, 0)
                if exists(b.plus(-1)):
                    back_mv(b.plus(-1))
                sum_of(b, 1)
                if exists(b.plus(1)):
                    front_q(b.plus(1))
                sum_of(b, 2)
                sum_of(b, 3)
                reciprocals(b)
                if exists(b.plus(1)):
                    front_kv(b.plus(1))
                if exists(b.plus(-1)):
                    back_z(b.plus(-1))
                if exists(b.plus(2)):
                    front_a(b.plus(2))
                normalise(b, 0)
                if exists(b.plus(-1)):
                    back_logits(b.plus(-1))

            batches(dve, B, before, body)
            last = Batch(0, B - 1)
            normalise(last, 1)
            back_x2(last)
            back_bn(last)
            back_mv(last)

            dve.wait_ge(pool_const, POOL_CONSTS)
            pe_of, pt_of = expert_of_p[:, 0:1], expert_of_p[:, 1:2]
            const(V.tensor_scalar(same_expert[:], col_expert[:], pe_of, None, ALU.is_equal))
            const(V.tensor_scalar(same_expert_f[:], col_expert[:], pe_of, None, ALU.is_equal))
            const(V.tensor_scalar(same_tile[:], col_tile[:], pt_of, None, ALU.is_equal))
            const(V.tensor_scalar(earlier_tile[:], col_tile[:], pt_of, None, ALU.is_gt))
            const(V.tensor_scalar(earlier_expert[:], col_expert[:], pe_of, None, ALU.is_gt), True)
            const(V.tensor_tensor(earlier_tile[:], earlier_tile[:], same_expert[:], ALU.mult))
            const(V.tensor_tensor(earlier_expert[:], earlier_expert[:], same_tile[:], ALU.mult))
            const(V.memset(zeros_row[:], 0.0))
            const(V.memset(order_rows[:], 0.0))
            for c in range(3):
                const(V.memset(flips[:, c:c + 1], c + 1))
            dve.wait_ge(dve_const, made[0])
            back_z(last)
            for r in range(15):
                const(V.tensor_scalar(digits[:, r], flips[:], 2 * (14 - r), None, ALU.logical_shift_left))
            dve.wait_ge(dve_const, made[0])
            back_logits(last)

            step = [0]

            def link(ins, then=True):
                ins.then_inc(dve_b, 1)
                step[0] += 1
                if then:
                    dve.wait_ge(dve_b, step[0])

            by_expert = [P, NT, E]

            def bc(a):
                return a.unsqueeze(2).to_broadcast(by_expert)

            dve.wait_ge(e_lg, B)
            for c in range(2):
                src = logits if c == 0 else rest
                link(V.tensor_reduce(top[:, c], src[:], AX.X, ALU.max))
                link(V.tensor_tensor(hit[:], src[:], bc(top[:, c]), ALU.is_equal))
                link(V.tensor_tensor(hit[:], hit[:], rank_weight[:], ALU.mult))
                link(V.tensor_reduce(first[:], hit[:], AX.X, ALU.max))
                link(V.tensor_tensor(chosen[:, c], rank_weight[:], bc(first[:]), ALU.is_equal))
                if c == 0:
                    link(V.scalar_tensor_tensor(rest[:], chosen[:, 0], -1e30, logits[:], ALU.mult, ALU.add))
            link(V.tensor_tensor(gap[:], top[:, 0], top[:, 1], ALU.subtract))
            V.tensor_tensor(pair[:, 0], chosen[:, 0], chosen[:, 1], ALU.add).then_inc(keys_ready, 1)
            link(V.tensor_tensor(pair[:, 1], chosen[:, 0], chosen[:, 1], ALU.subtract))
            dve.wait_ge(keys_ready, 1)
            link(V.tensor_tensor(pair[:, 1], pair[:, 1], bc(gap[:]), ALU.mult))
            link(V.tensor_scalar(pair[:, 1], pair[:, 1], SATURATED, GONE, ALU.min, ALU.max), False)
            link(V.tensor_scalar(pair[:, 2], pair[:, 0], -UNASSIGNED, UNASSIGNED, ALU.mult, ALU.add))
            V.tensor_tensor(keys[:], pair[:, 1], pair[:, 2], ALU.add).then_inc(keys_ready, 1)
            dve.wait_ge(e_ok, 1)
            link(V.tensor_scalar(gate_of[:, 1], gate_of[:, 0], 1.0, None, ALU.add))
            link(V.reciprocal(gate_of[:, 2], gate_of[:, 1]))
            link(V.tensor_tensor(gate_of[:, 3], gate_of[:, 0], gate_of[:, 2], ALU.mult), False)
            link(V.tensor_tensor(gates[:], chosen[:, 0], bc(gate_of[:, 2]), ALU.mult))
            link(V.tensor_tensor(pair[:, 0], chosen[:, 1], bc(gate_of[:, 3]), ALU.mult))
            V.tensor_tensor(gates[:], gates[:], pair[:, 0], ALU.add).then_inc(gates_ready, 1)

            by_pos = bank_b[:, P:2 * P].rearrange("p (t e) -> p t e", t=NT)

            def between_rounds(r):
                if r == 0:
                    link(V.tensor_scalar(junk[:, 3], keys_flat[:], UNASSIGNED / 2, 0.0, ALU.is_gt, ALU.add,
                                         accum_out=active[:, 0:1]), False)
                elif r == 1:
                    V.tensor_copy(active_bf[:], active[:, 0:1]).then_inc(active_step, 1)
                elif r == 2:
                    dve.wait_ge(active_sum, 1)
                    link(V.tensor_scalar(active[:, 1:2], small2[:, 0:1], 0.0, None, ALU.is_gt), False)
                elif r == 3:
                    V.tensor_copy(active_bf[:], active[:, 1:2]).then_inc(active_step, 1)
                elif r == 4:
                    dve.wait_ge(active_sum, 2)
                    link(V.tensor_copy(active[:, 2:4], small2[:, 0:2]), False)
                elif r == 5:
                    link(V.scalar_tensor_tensor(active[:, 4:5], pt_of, float(E), active[:, 2:3], ALU.mult, ALU.add), False)
                    link(V.tensor_scalar(order_rows[:, 0], col_index[0:E, 0:E], active[0:E, 2:3], active[0:E, 1:2],
                                         ALU.is_equal, ALU.mult), False)
                elif r == 6:
                    link(V.scalar_tensor_tensor(active[:, 4:5], active[:, 4:5], 1.0, active[:, 1:2], ALU.add, ALU.mult), False)
                    link(V.tensor_scalar(order_rows[:, 0], order_rows[:, 0], expert_of_p[0:E, 0:1], None, ALU.mult), False)
                elif r == 7:
                    link(V.tensor_scalar(active[:, 4:5], active[:, 4:5], -1.0, None, ALU.add), False)
                elif r == 8:
                    V.tensor_scalar(to_position[:], col_index[:], active[:, 4:5], None, ALU.is_equal).then_inc(active_step, 1)
                elif r == 9:
                    dve.wait_ge(active_sum, 3)
                    link(V.tensor_copy(order_i[0:1, 0:E], small2[0:1, 0:E]), False)
                    V.tensor_copy(order_i[0:1, E:E + 1], active[0:1, 3:4]).then_inc(order_ready, 1)
                elif r == 10:
                    dve.wait_ge(gate_pos_ps, 1)
                    dve.wait_ge(pool_const, POOL_CONSTS + 6)
                    link(V.tensor_copy(token_info[:, :, 0:E, 3], by_pos), False)
                elif r == 11:
                    link(V.tensor_tensor(gate_rest[:, 0], by_pos, token_info[:, :, 0:E, 3], ALU.subtract), False)
                elif r == 12:
                    link(V.tensor_copy(token_info[:, :, 0:E, 4], gate_rest[:, 0]), False)
                elif r == 13:
                    link(V.tensor_tensor(gate_rest[:, 1], gate_rest[:, 0], token_info[:, :, 0:E, 4], ALU.subtract), False)
                elif r == 14:
                    link(V.tensor_copy(token_info[:, :, 0:E, 5], gate_rest[:, 1]), False)

            V_first = (-(2.0 - 2.0 ** -23), 0.0, 2.0)
            dve.wait_ge(keys_ok, 1)
            for c in range(3):
                ins = V.tensor_scalar(junk[:, c], keys_flat[:], V_first[c], 0.0, ALU.is_ge, ALU.add,
                                      accum_out=counts[:, c:c + 1])
            ins.then_inc(counted, 1)
            dve.wait_ge(summed, 1)
            link(V.tensor_scalar(junk3[:], small[:, 0:3], float(CAP), 0.0, ALU.is_ge, ALU.add,
                                 accum_out=digit[:, 0:1]))
            link(V.tensor_scalar(prefix[:, 0:1], digit[:, 0:1], 2.0, -1.0, ALU.is_lt, ALU.mult), False)
            link(V.tensor_scalar(digit[:, 1:2], digit[:, 0:1], 1.0, None, ALU.is_equal), False)
            link(V.tensor_scalar(digit[:, 2:3], digit[:, 0:1], 3.0, None, ALU.is_equal))
            link(V.tensor_tensor(digit[:, 3:4], digit[:, 1:2], digit[:, 2:3], ALU.add))
            link(V.tensor_scalar(flips[:, 0:1], digit[:, 3:4], 2.0 ** 30, None, ALU.mult))
            link(V.tensor_tensor(prefix[:, 1:2], prefix[:, 0:1], flips[:, 0:1], ALU.bitwise_xor))
            link(V.tensor_tensor(candidates[:], digits[:, 0], prefix[:, 1:2].to_broadcast([P, 3]), ALU.bitwise_xor))
            ROUNDS = 15
            for r in range(ROUNDS):
                for c in range(3):
                    ins = V.tensor_scalar(junk[:, c], keys_flat[:], candidates[:, c:c + 1].bitcast(F32), 0.0,
                                          ALU.is_ge, ALU.add, accum_out=counts[:, c:c + 1])
                ins.then_inc(counted, 1)
                old, new = (r + 1) % 2, r % 2
                if r + 1 < ROUNDS:
                    link(V.tensor_tensor(next_prefix[:], digits[:, r + 1], prefix[:, old:old + 1].to_broadcast([P, 3]),
                                         ALU.bitwise_xor), False)
                between_rounds(r)
                dve.wait_ge(summed, 2 + r)
                link(V.tensor_scalar(junk3[:], small[:, 0:3], float(CAP), 0.0, ALU.is_ge, ALU.add,
                                     accum_out=digit[:, 0:1]))
                link(V.tensor_scalar(flips[:, 0:1], digit[:, 0:1], 2.0 ** (2 * (14 - r)), None, ALU.mult))
                if r + 1 < ROUNDS:
                    link(V.tensor_tensor(candidates[:], next_prefix[:], flips[:, 0:1].to_broadcast([P, 3]),
                                         ALU.bitwise_xor), False)
                link(V.tensor_tensor(prefix[:, new:new + 1], prefix[:, old:old + 1], flips[:, 0:1], ALU.bitwise_xor))
            threshold = prefix[:, (ROUNDS - 1) % 2:(ROUNDS - 1) % 2 + 1].bitcast(F32)

            link(V.tensor_scalar(above[:], keys_flat[:], threshold, 0.0, ALU.is_gt, ALU.add, accum_out=stats[:, 0:1]), False)
            link(V.tensor_scalar(equal[:], keys_flat[:], threshold, 0.0, ALU.is_equal, ALU.add, accum_out=stats[:, 1:2]), False)
            link(V.tensor_scalar(stats[:, 2:3], threshold, UNASSIGNED / 2, None, ALU.is_gt))
            V.tensor_copy(stats_bf[:, 0:2], stats[:, 0:2]).then_inc(counted, 1)
            dve.wait_ge(summed, 2 + ROUNDS)
            link(V.tensor_scalar(stats[:, 3:4], small[:, 0:1], -1.0, float(CAP), ALU.mult, ALU.add), False)
            link(V.tensor_copy(stats[:, 4:5], small[:, 1:2]))
            link(V.tensor_tensor(stats[:, 5:6], stats[:, 3:4], stats[:, 2:3], ALU.mult), False)
            link(V.tensor_tensor_scan(order_of[:], equal[:], zeros_row[:], stats[:, 4:5], ALU.add, ALU.add))
            link(V.scalar_tensor_tensor(taken[:], order_of[:], stats[:, 5:6], equal[:], ALU.is_le, ALU.mult))
            link(V.scalar_tensor_tensor(taken[:], taken[:], 1.0, above[:], ALU.mult, ALU.add, accum_out=stats[:, 6:7]))
            V.tensor_copy(stats_bf[:, 2:3], stats[:, 6:7]).then_inc(counted, 1)
            dve.wait_ge(summed, 3 + ROUNDS)
            link(V.tensor_copy(stats[:, 7:8], small[:, 0:1]))
            link(V.tensor_tensor_scan(order_of[:], taken[:], zeros_row[:], stats[:, 7:8], ALU.add, ALU.add))
            V.tensor_tensor(slot_flat[:], order_of[:], taken[:], ALU.mult).then_inc(counted, 1)

            dve.wait_ge(slot_pos_ps, 1)
            V.tensor_copy(slot_of[:, :, 0:E], bank_a[:, P:2 * P].rearrange("p (t e) -> p t e", t=NT)).then_inc(slot_pos_ok, 1)
            dve.wait_ge(slot_pos_ok, 1)

            def one_hots(i, par):
                if not isinstance(i, int):
                    dve.wait_ge(p_info, i - 1)
                for t in range(NT):
                    V.tensor_scalar(one_hot[:, par, t], slot_number[:], slot_of[:, t, bass.ds(i, 1)], None,
                                    ALU.is_equal).then_inc(s_hot, 1)

            def rows_of(i, par):
                dve.wait_ge(p_info, i + 1)
                V.tensor_copy(slot_info[:, par], bank_b[:, 0:6 * NM].rearrange("p (m c) -> p m c", c=6)).then_inc(e_info, 1)
                dve.wait_ge(e_info, i + 1)
                info = slot_info[:, par]
                if not isinstance(i, int):
                    dve.wait_ge(scattered, 16 * NM * (i - 1))
                    dve.wait_ge(s_y, NM * (i - 1))
                V.scalar_tensor_tensor(slot_calc[:, par, 0], info[:, :, 0], float(P), info[:, :, 1], ALU.mult, ALU.add).then_inc(s_calc, 1)
                V.tensor_scalar(slot_calc[:, par, 1], info[:, :, 2], -1.0, 1.0, ALU.mult, ALU.add).then_inc(s_calc, 1)
                V.tensor_tensor(slot_calc[:, par, 2], info[:, :, 3], info[:, :, 4], ALU.add).then_inc(s_calc, 1)
                dve.wait_ge(s_calc, 4 * i + 3)
                V.tensor_tensor(slot_calc[:, par, 1], slot_calc[:, par, 1], spare_row[:], ALU.mult).then_inc(s_calc, 1)
                V.tensor_copy(source_row[:, par], slot_calc[:, par, 0])
                V.tensor_tensor(slot_gate[:, par], slot_calc[:, par, 2], info[:, :, 5], ALU.add)
                dve.wait_ge(s_calc, 4 * i + 4)
                V.tensor_tensor(target_row[:, par], slot_calc[:, par, 0], slot_calc[:, par, 1], ALU.add).then_inc(s_rows, 1)

            for i in range(2):
                one_hots(i, i)
                rows_of(i, i)
            dve.sem_inc(e_y, NM)
            n_active = dve.value_load(order_i[0:1, E:E + 1], min_val=2, max_val=E)

            def weighted_rows(i, par, turn):
                for m, (_, rows) in enumerate(SLOTS):
                    dve.wait_ge(p_y, NM * i + m + 1)
                    dve.wait_ge(ld_bias[par], 32 * (turn + 1))
                    if m == 0:
                        dve.wait_ge(s_rows, i + 1)
                    V.tensor_tensor(y_b2[0:rows, m], y_ps[m][0:rows],
                                    b2_bc[0:rows, par], ALU.add).then_inc(e_y, 1)
                    dve.wait_ge(e_y, NM * (i + 1) + m + 1)
                    V.tensor_scalar(y_out[0:rows, par, m], y_b2[0:rows, m], slot_gate[0:rows, par, m:m + 1], None,
                                    ALU.mult).then_inc(s_y, 1)

            with dve.Fori(0, E // 2) as loop:
                even, odd = 2 * loop, 2 * loop + 1
                with dve.If(even < n_active):
                    with dve.If(even + 2 < n_active):
                        one_hots(even + 2, 0)
                    weighted_rows(even, 0, loop)
                    with dve.If(odd < n_active):
                        with dve.If(even + 2 < n_active):
                            rows_of(even + 2, 0)
                            with dve.If(odd + 2 < n_active):
                                one_hots(odd + 2, 1)
                        weighted_rows(odd, 1, loop)
                        with dve.If(odd + 2 < n_active):
                            rows_of(odd + 2, 1)

            def statistics(c):
                for b in (2 * c, 2 * c + 1):
                    dve.wait_ge(ld_acc[b], 16)
                    for t in range(T * b, T * b + T):
                        ins = V.bn_stats(bn3[:, t], acc[:, t])
                ins.then_inc(d_bn, 1)
                dve.wait_ge(d_bn, c + 1)
                for t in range(2 * T * c, 2 * T * (c + 1)):
                    ins = V.bn_aggr(mv3[:, t], bn3[:, t])
                ins.then_inc(d_mv, 1)

            def bias_pair(c):
                tiles = slice(2 * T * c, 2 * T * (c + 1))
                dve.wait_ge(d_rs, c + 1)
                V.scalar_tensor_tensor(nb3[:, tiles], mv3[:, tiles, 0], -1.0, rs3[:, tiles], ALU.mult, ALU.mult).then_inc(d_nb, 1)

            def finish(b):
                tiles = slice(T * b, T * b + T)
                if b in OWN:
                    dve.wait_ge(d_norm, b + 1)
                    V.tensor_tensor(scaled[:, tiles], acc[:, tiles], gamma_bc[:].unsqueeze(1).to_broadcast([P, T, D]),
                                    ALU.mult).then_inc(d_own_gamma, 1)
                    dve.wait_ge(d_own_gamma, OWN.index(b) + 1)
                else:
                    dve.wait_ge(d_gamma, SHARED.index(b) + 1)
                V.tensor_tensor(acc[:, tiles], scaled[:, tiles], x2_beta[:, tiles], ALU.add).then_inc(d_res, 1)

            statistics(0)
            statistics(1)
            bias_pair(0)
            statistics(2)
            bias_pair(1)
            statistics(3)
            bias_pair(2)
            finish(FINISHED[0])
            bias_pair(3)
            for b in FINISHED[1:]:
                finish(b)

        @block.tensor
        def _(pe):
            def mm(out_, lhs, rhs, start=True, stop=True):
                return nc.tensor.matmul(out_, lhs, rhs, start=start, stop=stop, skip_group_check=True)

            def tr(out_, in_, identity):
                return nc.tensor.transpose(out_, in_, identity)

            pe.wait_ge(ld_w[0], 32)
            pe.wait_ge(pool_const, FIRST_CONSTS)
            tr(bank_a[:, 0:4], bqk_rows[:, :], ident[0:4, 0:4]).then_inc(bqk_ps, 1)
            pe.wait_ge(act_const, 1)

            def front_ctx(b):
                wait(pe, e_o, G * (b.n - 1))
                pe.wait_ge(ld_ctx[b.par], 16 * (b.turn + 1))
                for k in range(KD):
                    tr(bank_b[:, k * SK:(k + 1) * SK], ctx_in[:, b.par, k * P:(k + 1) * P], ident[0:SK, 0:SK])
                pe.wait_ge(s_quarter, b.n + 1)
                for t in range(T):
                    ins = mm(bank_b[:, S + t * P:S + (t + 1) * P], quarter[:, t:t + 1].to_broadcast([P, P]), ident_bf[:])
                ins.then_inc(p_ctx, 1)

            def front_xn(b):
                if isinstance(b.n, int) and b.n == 0:
                    pe.wait_ge(bqk_ok, 1)
                elif isinstance(b.n, int) and b.n == 1:
                    pe.wait_ge(e_q, G)
                else:
                    pe.wait_ge(e_x2, b.n - 1)
                pe.wait_ge(s_xn, b.n + 1)
                for k in range(KD):
                    for t in range(T):
                        ins = tr(bank_a[:, k * S + t * P:k * S + (t + 1) * P], xn[:, t, k * P:(k + 1) * P], ident[:])
                ins.then_inc(p_xnt, 1)

            def front_q(b, g):
                if g == 0:
                    pe.wait_ge(ld_wq, 16)
                    if isinstance(b.n, int) and b.n == 0:
                        pe.wait_ge(e_kv, 4)
                    pe.wait_ge(e_xnt, b.n + 1)
                for k in range(KD):
                    ins = mm(bank_a[:, g * S:(g + 1) * S], wq_sb[:, k, g * P:(g + 1) * P], xn_t[:, k],
                             start=k == 0, stop=k == KD - 1)
                if g == G - 1:
                    ins.then_inc(p_q, 1)

            def front_k(b):
                if isinstance(b.n, int) and b.n == 0:
                    pe.wait_ge(e_xnt, 1)
                else:
                    pe.wait_ge(e_q, G * (b.n + 1))
                pe.wait_ge(e_ctx, 2 * (b.n + 1))
                pe.wait_ge(ld_w[1], 16)
                for g in range(G):
                    for k in range(KD):
                        mm(bank_a[:, g * SK:(g + 1) * SK], wk_sb[:, k, g * P:(g + 1) * P], ctx_t[:, k],
                           start=k == 0, stop=k == KD - 1)

            def front_v(b):
                pe.wait_ge(ld_w[2], 32)
                for k in range(KD):
                    ins = mm(bank_a[0:SK, S:2 * S], ctx_t[:, k], wv_sb[:, k], start=k == 0, stop=k == KD - 1)
                ins.then_inc(p_kv, 1)

            def scores(b, k):
                g, t = k // T, k % T
                wait(pe, s_sub, 4 * b.n + k - 1)
                if k == 0:
                    wait(pe, e_q, G * (b.n + 1))
                    wait(pe, s_heads, b.n + 1)
                    wait(pe, s_mask, T * (b.n + 1))
                for half in range(2):
                    mm(score_ps[:, k % 2, half, 0:4 * SK], ident_bf[:],
                       mask_bf[:, b.par, t].unsqueeze(1).to_broadcast([P, 4, SK]), stop=False)
                for half in range(2):
                    first = g * (H // G) + 4 * half
                    ins = mm(score_ps[:, k % 2, half, 0:4 * SK], q_t[:, b.par, g, t * P:(t + 1) * P],
                             k_heads[:, b.par, first:first + 4].rearrange("p h k -> p (h k)"), start=False)
                ins.then_inc(p_scores, 1)

            def transpose_probs(b, g, j):
                pe.wait_ge(e_exp, 4 * b.n + T * (g + 1))
                wait(pe, e_probs, H // 2 * b.n + J * g + j - 1)
                for s in range(2):
                    for t in range(T):
                        ins = tr(probs_ps[0:SK, j % 2, s * S + t * P:s * S + (t + 1) * P],
                                 probs_q[:, g, t, j // 2, 2 * (j % 2) + s], ident[:])
                ins.then_inc(p_probs, 1)

            def transpose_recip(b):
                pe.wait_ge(s_recip, b.n + 1)
                pe.wait_ge(e_ctx, ctx_count(b))
                for t in range(T):
                    ins = tr(bank_b[0:H, t * P:(t + 1) * P], recip[:, t], ident[:])
                ins.then_inc(p_recip, 1)

            def spread_recip(b):
                pe.wait_ge(e_recip, b.n + 1)
                if isinstance(b.n, int) and b.n == 0:
                    pe.wait_ge(pool_const, POOL_CONSTS)
                for g in range(G):
                    ins = mm(bank_b[:, g * S:(g + 1) * S], head_columns[:, g], recip_t[:])
                ins.then_inc(p_rows, 1)

            def ctx_count(b):
                return 2 * min(b.n + 2, B) if isinstance(b.n, int) else 2 * (b.n + 2)

            def weighted_values(b, g):
                if g == 0:
                    pe.wait_ge(e_rows, b.n + 1)
                else:
                    pe.wait_ge(e_o, G * b.n + 1)
                pe.wait_ge(e_probs, H // 2 * b.n + J * (g + 1))
                for s in range(2):
                    for j in range(J):
                        ins = mm(bank_b[RB * j:RB * (j + 1), g * S:(g + 1) * S], v_pad[:, b.par, 8 * g + 2 * j + s],
                                 probs[0:SK, g, j, s], start=s == 0, stop=s == 1)
                ins.then_inc(p_pv, 1)

            def back_o(b):
                if isinstance(b.n, int) and b.n == 0:
                    pe.wait_ge(e_kv, 4 * 2)
                else:
                    pe.wait_ge(e_lg, b.n)
                pe.wait_ge(e_o, G * (b.n + 1))
                pe.wait_ge(ld_w[3], 32)
                for t in range(T):
                    for g in range(G):
                        ins = mm(bank_a[:, t * D:(t + 1) * D], o_t[:, g, t * P:(t + 1) * P], wo_sb[:, g],
                                 start=g == 0, stop=g == G - 1)
                ins.then_inc(p_o, 1)

            def back_z(b):
                if is_last_batch(b) or is_last_batch(b.plus(1)):
                    pe.wait_ge(e_x2, b.n + 1)
                else:
                    pe.wait_ge(e_kv, 4 * (b.n + 3))
                pe.wait_ge(e_z, b.n + 1)
                for k in range(KD):
                    for t in range(T):
                        ins = tr(bank_a[:, k * S + t * P:k * S + (t + 1) * P], z[:, t, k * P:(k + 1) * P], ident[:])
                ins.then_inc(p_zt, 1)

            def back_logits(b):
                pe.wait_ge(e_zt, b.n + 1)
                pe.wait_ge(ld_w[4], 64)
                for t in range(T):
                    for k in range(KD):
                        ins = mm(bank_a[:, t * E:(t + 1) * E], z_t[:, k, t * P:(t + 1) * P], wr_sb[:, k],
                                 start=k == 0, stop=k == KD - 1)
                ins.then_inc(p_lg, 1)

            def is_last_batch(b):
                return isinstance(b.n, int) and b.n == B - 1

            def before(b):
                front_ctx(b)
                front_xn(b)
                front_k(b)
                front_v(b)
                for g in range(G):
                    front_q(b, g)

            def body(b):
                scores(b, 0)
                scores(b, 1)
                if exists(b.plus(-1)):
                    weighted_values(b.plus(-1), 1)
                scores(b, 2)
                if exists(b.plus(-1)):
                    back_o(b.plus(-1))
                scores(b, 3)
                if exists(b.plus(1)):
                    front_ctx(b.plus(1))
                    front_xn(b.plus(1))
                transpose_probs(b, 0, 0)
                transpose_probs(b, 0, 1)
                if exists(b.plus(1)):
                    front_q(b.plus(1), 0)
                transpose_probs(b, 0, 2)
                if exists(b.plus(1)):
                    front_q(b.plus(1), 1)
                transpose_probs(b, 0, 3)
                transpose_probs(b, 1, 0)
                if exists(b.plus(1)):
                    front_k(b.plus(1))
                transpose_probs(b, 1, 1)
                if exists(b.plus(1)):
                    front_v(b.plus(1))
                transpose_recip(b)
                transpose_probs(b, 1, 2)
                spread_recip(b)
                if exists(b.plus(-1)):
                    back_z(b.plus(-1))
                transpose_probs(b, 1, 3)
                weighted_values(b, 0)
                if exists(b.plus(-1)):
                    back_logits(b.plus(-1))

            batches(pe, B, before, body)
            last = Batch(0, B - 1)
            weighted_values(last, 1)
            back_o(last)
            back_z(last)
            back_logits(last)

            flat = "p t e -> p (t e)"
            pe.wait_ge(keys_ready, 2)
            pe.wait_ge(e_lg, B)
            tr(bank_a[:, 0:P], keys[:].rearrange(flat), ident[:]).then_inc(keys_ps, 1)
            pe.wait_ge(gates_ready, 1)
            pe.wait_ge(e_lg, B)
            tr(bank_b[:, 0:P], gates[:].rearrange(flat), ident[:]).then_inc(gates_ps, 1)
            for r in range(-1, 15):
                pe.wait_ge(counted, r + 2)
                mm(small[:, 0:3], same_expert_f[:], counts[:]).then_inc(summed, 1)
                if r == 1:
                    pe.wait_ge(active_step, 1)
                    mm(small2[:, 0:1], same_expert[:], active_bf[:]).then_inc(active_sum, 1)
                elif r == 3:
                    pe.wait_ge(active_step, 2)
                    mm(small2[:, 0:1], earlier_expert[:], active_bf[:])
                    mm(small2[:, 1:2], same_tile[:], active_bf[:]).then_inc(active_sum, 1)
                elif r == 8:
                    pe.wait_ge(active_step, 3)
                    mm(small2[0:1, 0:E], ones[0:E], order_rows[:, 0]).then_inc(active_sum, 1)
                    pe.wait_ge(gates_ok, 1)
                    mm(bank_b[:, P:2 * P], gates_flat[:], to_position[:]).then_inc(gate_pos_ps, 1)
            pe.wait_ge(counted, 17)
            mm(small[:, 0:1], same_expert[:], stats_bf[:, 0:1])
            mm(small[:, 1:2], earlier_tile[:], stats_bf[:, 1:2]).then_inc(summed, 1)
            pe.wait_ge(counted, 18)
            mm(small[:, 0:1], earlier_tile[:], stats_bf[:, 2:3]).then_inc(summed, 1)
            pe.wait_ge(counted, 19)
            mm(bank_a[:, P:2 * P], slot_flat[:], to_position[:]).then_inc(slot_pos_ps, 1)

            def slot_map(i, par):
                if not isinstance(i, int) or i > 0:
                    pe.wait_ge(e_info, i)
                for t in range(NT):
                    pe.wait_ge(s_hot, NT * i + t + 1)
                    for m, (at, rows) in enumerate(SLOTS):
                        ins = mm(bank_b[0:rows, 6 * m:6 * m + 6], one_hot[:, par, t, at:at + rows],
                                 token_info[:, t, bass.ds(i, 1)].rearrange("p a c -> p (a c)"),
                                 start=t == 0 and m == 0, stop=t == NT - 1)
                ins.then_inc(p_info, 1)

            slot_map(0, 0)
            slot_map(1, 1)
            pe.wait_ge(e_info, 2)

            def rows_transposed(i, par, turn):
                pe.wait_ge(ld_bias[par], 32 * (turn + 1))
                for m in range(NM):
                    pe.wait_ge(gathered[par][m], 16 * (turn + 1))
                for m, (at, rows) in enumerate(SLOTS):
                    for k, bank in enumerate((bank_a, bank_b)):
                        tr(bank[:, at:at + rows], xe[0:rows, par, m, k * P:(k + 1) * P], ident[0:rows, 0:rows])
                tr(bank_a[:, CAP:CAP + KF], b1_rows[:, par], ident[0:KF, 0:KF]).then_inc(p_xe, 1)

            rows_transposed(0, 0, 0)
            n_active = pe.value_load(order_i[0:1, E:E + 1], min_val=2, max_val=E)
            with pe.Fori(0, E // 2) as loop:
                for par in range(2):
                    i = 2 * loop + par
                    with pe.If(i < n_active):
                        pe.wait_ge(e_xe, 3 * (i + 1))
                        pe.wait_ge(ld_w1[par], 16 * (loop + 1))
                        for f in range(KF):
                            if f >= NH:
                                pe.wait_ge(e_h, KF * i + f - NH + 1)
                            for k in range(KD):
                                ins = mm(h_ps[:, f % NH, 0:CAP], w1_sb[:, par, k, f * P:(f + 1) * P], xe_t[:, k],
                                         start=k == 0, stop=k == KD - 1)
                            ins.then_inc(p_h, 1)
                    with pe.If(i + 1 < n_active):
                        rows_transposed(i + 1, 1 - par, loop + par)
                    with pe.If(i < n_active):
                        pe.wait_ge(ld_w2[par], 16 * (loop + 1))
                        pe.wait_ge(e_y, NM * (i + 1))
                        for m, (at, rows) in enumerate(SLOTS):
                            if m == 2:
                                pe.wait_ge(e_y, NM * (i + 1) + 1)
                            for f in range(KF):
                                if m == 0:
                                    pe.wait_ge(e_h, KF * i + f + 1)
                                ins = mm(y_ps[m][0:rows], hidden[:, f, at:at + rows],
                                         w2_sb[:, par, f], start=f == 0, stop=f == KF - 1)
                            ins.then_inc(p_y, 1)
                    with pe.If(i + 2 < n_active):
                        pe.wait_ge(e_xe, 3 * (i + 2))
                        slot_map(i + 2, par)
                        pe.wait_ge(e_info, i + 3)


_INS = ["x", "ctx_1024", "mask_BxSxS2_ik1",
        "L0_xattn_wq_kernel", "L0_xattn_wq_bias", "L0_xattn_wk_kernel", "L0_xattn_wk_bias",
        "L0_xattn_wv_kernel", "L0_xattn_wv_bias", "L0_xattn_wo_kernel", "L0_xattn_wo_bias",
        "L0_ffn_Wr", "L0_ffn_br", "L0_ffn_W1", "L0_ffn_b1", "L0_ffn_W2", "L0_ffn_b2",
        "L0_ffn_gamma", "L0_ffn_beta"]


def kernel(**inputs):
    import numpy as _np
    import concourse.bacc as _bacc
    from concourse import mybir as _mybir
    from concourse.bass_utils import run_bass_kernel_spmd as _run

    nc = _bacc.Bacc("TRN2", target_bir_lowering=False, num_devices=1)
    arrays, args = {}, []
    for name in _INS:
        a = _np.ascontiguousarray(inputs[name])
        arrays[f"in_{name}"] = a
        args.append(nc.dram_tensor(f"in_{name}", a.shape, _mybir.dt.from_np(a.dtype), kind="ExternalInput").ap())
    shape = tuple(inputs["x"].shape)
    args.append(nc.dram_tensor("out_0", shape, _mybir.dt.float32, kind="ExternalOutput").ap())
    xattn_moe(nc, *args)
    r = _run(nc, [arrays], core_ids=[0])
    return r.results[0]["out_0"]
```
